# Optimizing a Trainium2 kernel written in Bass

```python
import numpy as np
import jax
import jax.numpy as jnp

def _softmax(x, axis=-1):
    return jax.nn.softmax(x, axis=axis)

def _gelu(x):
    return jax.nn.gelu(x, approximate=True)

def _silu(x):
    return jax.nn.silu(x)

def _sigmoid(x):
    return jax.nn.sigmoid(x)

def _layernorm(x, axis=-1, eps=1e-05):
    m = jnp.mean(x, axis=axis, keepdims=True)
    v = jnp.var(x, axis=axis, keepdims=True)
    return (x - m) / jnp.sqrt(v + eps)

def _scatter_add(tgt, idx, src, axis=0):
    return tgt.at[idx].add(src)

def _segment_sum(src, seg, n):
    return jax.ops.segment_sum(src, seg, n)
kernel_name = 'mk_gnn_preln_d4_gnn_r8_669205'

def setup_inputs(seed: int=0):
    np.random.seed(seed)
    _w = jnp.asarray

    def _rec_inputs():
        import jax
        import jax.numpy as jnp
        _gk = jax.random.key(seed)
        x = -0.000202 + 1 * jax.random.normal(jax.random.fold_in(_gk, 1), (12500, 128), jnp.float32)
        _s = jax.random.randint(jax.random.fold_in(_gk, 2), (100000,), 0, 12500, jnp.int32)
        _d = jax.random.randint(jax.random.fold_in(_gk, 3), (100000,), 0, 12500, jnp.int32)
        _loop = jnp.arange(12500, dtype=jnp.int32)
        src = jnp.concatenate([_s, _d, _loop])
        dst = jnp.concatenate([_d, _s, _loop])
        _o = jnp.argsort(dst, stable=True)
        src = src[_o]
        dst = dst[_o]
        edge_weight = jax.random.uniform(jax.random.fold_in(_gk, 13), (212500,), jnp.float32, 0.0, 1)
        return (x, src, dst, edge_weight)
    x, src, dst, edge_weight = _rec_inputs()

    def _L0_gnn_setup():
        import jax, jax.numpy as jnp
        import numpy as np
        NEG_SLOPE = 0.2
        EPS = 1e-16

        def gat_conv(x, src, dst, W, a_src, a_dst, b, n_nodes):
            h = x @ W
            alpha_src = h @ a_src
            alpha_dst = h @ a_dst
            e = jax.nn.leaky_relu(alpha_src[src] + alpha_dst[dst], NEG_SLOPE)
            m = jax.ops.segment_max(e, dst, num_segments=n_nodes)
            ex = jnp.exp(e - m[dst])
            s = jax.ops.segment_sum(ex, dst, num_segments=n_nodes)
            alpha = ex / (s[dst] + EPS)
            out = jax.ops.segment_sum(alpha[:, None] * h[src], dst, num_segments=n_nodes)
            return out + b
        key = jax.random.key(seed)
        ks = jax.random.split(key, 10)
        N, E, C_IN, HID, C_OUT = (6250, 150000, 128, 64, 128)
        x = jax.random.normal(ks[0], (N, C_IN), dtype=jnp.float32)
        edge_index = jax.random.randint(ks[1], (2, E), 0, N, dtype=jnp.int64)
        W1 = jax.random.normal(ks[2], (C_IN, HID), dtype=jnp.float32) / np.sqrt(C_IN)
        a_src1 = jax.random.normal(ks[3], (HID,), dtype=jnp.float32) / np.sqrt(HID)
        a_dst1 = jax.random.normal(ks[4], (HID,), dtype=jnp.float32) / np.sqrt(HID)
        b1 = jnp.zeros((HID,), dtype=jnp.float32)
        W2 = jax.random.normal(ks[5], (HID, C_OUT), dtype=jnp.float32) / np.sqrt(HID)
        a_src2 = jax.random.normal(ks[6], (C_OUT,), dtype=jnp.float32) / np.sqrt(C_OUT)
        a_dst2 = jax.random.normal(ks[7], (C_OUT,), dtype=jnp.float32) / np.sqrt(C_OUT)
        b2 = jnp.zeros((C_OUT,), dtype=jnp.float32)
        return {'x': x, 'edge_index': edge_index, 'W1': W1, 'a_src1': a_src1, 'a_dst1': a_dst1, 'b1': b1, 'W2': W2, 'a_src2': a_src2, 'a_dst2': a_dst2, 'b2': b2}
    _L0_gnn_all = _L0_gnn_setup()
    _L0_gnn_in = {k: v for k, v in _L0_gnn_all.items() if k in ('W1', 'a_src1', 'a_dst1', 'b1', 'W2', 'a_src2', 'a_dst2', 'b2')}
    del _L0_gnn_all

    def _L1_gnn_setup():
        import jax, jax.numpy as jnp
        import numpy as np
        N = 6250
        E = 80000
        DM = 128
        H = 8
        HD = DM // H
        FF = 512
        EPS = 1e-05

        def layer_norm(x, g, b):
            mu = jnp.mean(x, axis=-1, keepdims=True)
            var = jnp.mean(jnp.square(x - mu), axis=-1, keepdims=True)
            return (x - mu) * jax.lax.rsqrt(var + EPS) * g + b

        def transformer_conv(x, src, dst, Wq, bq, Wk, bk, Wv, bv, Wskip, bskip):
            n = x.shape[0]
            q = (x @ Wq + bq).reshape(n, H, HD)
            k = (x @ Wk + bk).reshape(n, H, HD)
            v = (x @ Wv + bv).reshape(n, H, HD)
            alpha = jnp.einsum('ehd,ehd->eh', q[dst], k[src]) / jnp.float32(np.sqrt(HD))
            m = jax.ops.segment_max(alpha, dst, num_segments=n)
            ex = jnp.exp(alpha - m[dst])
            den = jax.ops.segment_sum(ex, dst, num_segments=n) + 1e-16
            a = ex / den[dst]
            agg = jax.ops.segment_sum(a[:, :, None] * v[src], dst, num_segments=n)
            return agg.reshape(n, DM) + x @ Wskip + bskip
        key = jax.random.key(seed)
        ks = jax.random.split(key, 16)
        w = lambda k, sh: jax.random.normal(k, sh, jnp.float32) * 0.02
        return {'x': jax.random.normal(ks[0], (N, DM), jnp.float32), 'edge_index': jax.random.randint(ks[1], (2, E), 0, N, dtype=jnp.int32).astype(jnp.int64), 'Wq': w(ks[2], (DM, DM)), 'bq': jnp.zeros((DM,), jnp.float32), 'Wk': w(ks[3], (DM, DM)), 'bk': jnp.zeros((DM,), jnp.float32), 'Wv': w(ks[4], (DM, DM)), 'bv': jnp.zeros((DM,), jnp.float32), 'Wskip': w(ks[5], (DM, DM)), 'bskip': jnp.zeros((DM,), jnp.float32), 'Wo': w(ks[6], (DM, DM)), 'bo': jnp.zeros((DM,), jnp.float32), 'g1': jnp.ones((DM,), jnp.float32), 'b1': jnp.zeros((DM,), jnp.float32), 'Wf1': w(ks[7], (DM, FF)), 'bf1': jnp.zeros((FF,), jnp.float32), 'Wf2': w(ks[8], (FF, DM)), 'bf2': jnp.zeros((DM,), jnp.float32), 'g2': jnp.ones((DM,), jnp.float32), 'b2': jnp.zeros((DM,), jnp.float32)}
    _L1_gnn_all = _L1_gnn_setup()
    _L1_gnn_in = {k: v for k, v in _L1_gnn_all.items() if k in ('Wq', 'bq', 'Wk', 'bk', 'Wv', 'bv', 'Wskip', 'bskip', 'Wo', 'bo', 'g1', 'b1', 'Wf1', 'bf1', 'Wf2', 'bf2', 'g2', 'b2')}
    del _L1_gnn_all

    def _L2_gnn_setup():
        import jax, jax.numpy as jnp
        import numpy as np
        N_NODES = 6250
        N_EDGES = 100000
        HID = 128
        key = jax.random.key(seed)
        ks = jax.random.split(key, 10)
        s_msg = 1.0 / np.sqrt(2 * HID + 1)
        s_u1 = 1.0 / np.sqrt(2 * HID)
        s_u2 = 1.0 / np.sqrt(HID)
        return {'z': jax.random.normal(ks[0], (N_NODES, HID), dtype=jnp.float32), 'edge_weight': jax.random.uniform(ks[1], (N_EDGES,), dtype=jnp.float32), 'edge_src': jax.random.randint(ks[2], (N_EDGES,), 0, N_NODES), 'edge_dst': jax.random.randint(ks[3], (N_EDGES,), 0, N_NODES), 'Wm': jax.random.normal(ks[4], (2 * HID + 1, HID), dtype=jnp.float32) * s_msg, 'bm': jax.random.normal(ks[5], (HID,), dtype=jnp.float32) * s_msg, 'W1': jax.random.normal(ks[6], (2 * HID, HID), dtype=jnp.float32) * s_u1, 'b1': jax.random.normal(ks[7], (HID,), dtype=jnp.float32) * s_u1, 'W2': jax.random.normal(ks[8], (HID, HID), dtype=jnp.float32) * s_u2, 'b2': jax.random.normal(ks[9], (HID,), dtype=jnp.float32) * s_u2}
    _L2_gnn_all = _L2_gnn_setup()
    _L2_gnn_in = {k: v for k, v in _L2_gnn_all.items() if k in ('Wm', 'bm', 'W1', 'b1', 'W2', 'b2')}
    del _L2_gnn_all

    def _L3_gnn_setup():
        import jax, jax.numpy as jnp
        import numpy as np
        N_NODES = 12500
        key = jax.random.key(seed)
        k1, k2, k3 = jax.random.split(key, 3)
        x = jax.random.normal(k1, (N_NODES, 128), dtype=jnp.float32)
        edge_src = jax.random.randint(k2, (80000,), 0, N_NODES, dtype=jnp.int64)
        edge_dst = jax.random.randint(k3, (80000,), 0, N_NODES, dtype=jnp.int64)
        return {'x': x, 'edge_src': edge_src, 'edge_dst': edge_dst}
    _L3_gnn_all = _L3_gnn_setup()
    _L3_gnn_in = {k: v for k, v in _L3_gnn_all.items() if k in ()}
    del _L3_gnn_all
    return {'x': x, 'src': src, 'dst': dst, 'edge_weight': edge_weight, 'L0_gnn_W1': _L0_gnn_in['W1'], 'L0_gnn_a_src1': _L0_gnn_in['a_src1'], 'L0_gnn_a_dst1': _L0_gnn_in['a_dst1'], 'L0_gnn_b1': _L0_gnn_in['b1'], 'L0_gnn_W2': _L0_gnn_in['W2'], 'L0_gnn_a_src2': _L0_gnn_in['a_src2'], 'L0_gnn_a_dst2': _L0_gnn_in['a_dst2'], 'L0_gnn_b2': _L0_gnn_in['b2'], 'L1_gnn_Wq': _L1_gnn_in['Wq'], 'L1_gnn_bq': _L1_gnn_in['bq'], 'L1_gnn_Wk': _L1_gnn_in['Wk'], 'L1_gnn_bk': _L1_gnn_in['bk'], 'L1_gnn_Wv': _L1_gnn_in['Wv'], 'L1_gnn_bv': _L1_gnn_in['bv'], 'L1_gnn_Wskip': _L1_gnn_in['Wskip'], 'L1_gnn_bskip': _L1_gnn_in['bskip'], 'L1_gnn_Wo': _L1_gnn_in['Wo'], 'L1_gnn_bo': _L1_gnn_in['bo'], 'L1_gnn_g1': _L1_gnn_in['g1'], 'L1_gnn_b1': _L1_gnn_in['b1'], 'L1_gnn_Wf1': _L1_gnn_in['Wf1'], 'L1_gnn_bf1': _L1_gnn_in['bf1'], 'L1_gnn_Wf2': _L1_gnn_in['Wf2'], 'L1_gnn_bf2': _L1_gnn_in['bf2'], 'L1_gnn_g2': _L1_gnn_in['g2'], 'L1_gnn_b2': _L1_gnn_in['b2'], 'L2_gnn_Wm': _L2_gnn_in['Wm'], 'L2_gnn_bm': _L2_gnn_in['bm'], 'L2_gnn_W1': _L2_gnn_in['W1'], 'L2_gnn_b1': _L2_gnn_in['b1'], 'L2_gnn_W2': _L2_gnn_in['W2'], 'L2_gnn_b2': _L2_gnn_in['b2']}

def reference(x, src, dst, edge_weight, L0_gnn_W1, L0_gnn_a_src1, L0_gnn_a_dst1, L0_gnn_b1, L0_gnn_W2, L0_gnn_a_src2, L0_gnn_a_dst2, L0_gnn_b2, L1_gnn_Wq, L1_gnn_bq, L1_gnn_Wk, L1_gnn_bk, L1_gnn_Wv, L1_gnn_bv, L1_gnn_Wskip, L1_gnn_bskip, L1_gnn_Wo, L1_gnn_bo, L1_gnn_g1, L1_gnn_b1, L1_gnn_Wf1, L1_gnn_bf1, L1_gnn_Wf2, L1_gnn_bf2, L1_gnn_g2, L1_gnn_b2, L2_gnn_Wm, L2_gnn_bm, L2_gnn_W1, L2_gnn_b1, L2_gnn_W2, L2_gnn_b2):
    import jax
    import jax.numpy as jnp

    def _L0_gnn_ref(x, edge_index, W1, a_src1, a_dst1, b1, W2, a_src2, a_dst2, b2):
        import jax, jax.numpy as jnp
        import numpy as np
        NEG_SLOPE = 0.2
        EPS = 1e-16

        def gat_conv(x, src, dst, W, a_src, a_dst, b, n_nodes):
            h = x @ W
            alpha_src = h @ a_src
            alpha_dst = h @ a_dst
            e = jax.nn.leaky_relu(alpha_src[src] + alpha_dst[dst], NEG_SLOPE)
            m = jax.ops.segment_max(e, dst, num_segments=n_nodes)
            ex = jnp.exp(e - m[dst])
            s = jax.ops.segment_sum(ex, dst, num_segments=n_nodes)
            alpha = ex / (s[dst] + EPS)
            out = jax.ops.segment_sum(alpha[:, None] * h[src], dst, num_segments=n_nodes)
            return out + b
        n_nodes = x.shape[0]
        loops = jnp.arange(n_nodes, dtype=edge_index.dtype)
        src = jnp.concatenate([edge_index[0], loops])
        dst = jnp.concatenate([edge_index[1], loops])
        h = jax.nn.relu(gat_conv(x, src, dst, W1, a_src1, a_dst1, b1, n_nodes))
        return gat_conv(h, src, dst, W2, a_src2, a_dst2, b2, n_nodes)

    def _L1_gnn_ref(x, edge_index, Wq, bq, Wk, bk, Wv, bv, Wskip, bskip, Wo, bo, g1, b1, Wf1, bf1, Wf2, bf2, g2, b2):
        import jax, jax.numpy as jnp
        import numpy as np
        N = 6250
        E = 80000
        DM = 128
        H = 8
        HD = DM // H
        FF = 512
        EPS = 1e-05

        def layer_norm(x, g, b):
            mu = jnp.mean(x, axis=-1, keepdims=True)
            var = jnp.mean(jnp.square(x - mu), axis=-1, keepdims=True)
            return (x - mu) * jax.lax.rsqrt(var + EPS) * g + b

        def transformer_conv(x, src, dst, Wq, bq, Wk, bk, Wv, bv, Wskip, bskip):
            n = x.shape[0]
            q = (x @ Wq + bq).reshape(n, H, HD)
            k = (x @ Wk + bk).reshape(n, H, HD)
            v = (x @ Wv + bv).reshape(n, H, HD)
            alpha = jnp.einsum('ehd,ehd->eh', q[dst], k[src]) / jnp.float32(np.sqrt(HD))
            m = jax.ops.segment_max(alpha, dst, num_segments=n)
            ex = jnp.exp(alpha - m[dst])
            den = jax.ops.segment_sum(ex, dst, num_segments=n) + 1e-16
            a = ex / den[dst]
            agg = jax.ops.segment_sum(a[:, :, None] * v[src], dst, num_segments=n)
            return agg.reshape(n, DM) + x @ Wskip + bskip
        src = edge_index[0]
        dst = edge_index[1]
        conv = transformer_conv(x, src, dst, Wq, bq, Wk, bk, Wv, bv, Wskip, bskip)
        out1 = conv @ Wo + bo
        out2 = layer_norm(out1 + x, g1, b1)
        out3 = jax.nn.relu(out2 @ Wf1 + bf1) @ Wf2 + bf2
        out4 = layer_norm(out3 + out2, g2, b2)
        return out4

    def _L2_gnn_ref(z, edge_weight, edge_src, edge_dst, Wm, bm, W1, b1, W2, b2):
        import jax, jax.numpy as jnp
        import numpy as np
        N_NODES = 6250
        N_EDGES = 100000
        HID = 128
        n, H = z.shape
        Wd, Ws, ww = (Wm[:H], Wm[H:2 * H], Wm[2 * H])
        msgs = z[edge_dst] @ Wd + z[edge_src] @ Ws + edge_weight[:, None] * ww[None, :] + bm
        agg = jax.ops.segment_max(msgs, edge_dst, num_segments=n)
        deg = jax.ops.segment_sum(jnp.ones_like(edge_weight), edge_dst, num_segments=n)
        agg = jnp.where(deg[:, None] > 0, agg, jnp.zeros((), dtype=z.dtype))
        W1a, W1b = (W1[:H], W1[H:])
        hidden = jax.nn.relu(z @ W1a + agg @ W1b + b1)
        return hidden @ W2 + b2

    def _L3_gnn_ref(x, edge_src, edge_dst):
        import jax, jax.numpy as jnp
        import numpy as np
        N_NODES = 12500
        n = x.shape[0]
        gathered = x[edge_src]
        sums = jax.ops.segment_sum(gathered, edge_dst, num_segments=n)
        counts = jax.ops.segment_sum(jnp.ones(edge_dst.shape, dtype=x.dtype), edge_dst, num_segments=n)
        denom = jnp.maximum(counts, 1.0)[:, None]
        return sums / denom
    edge_index = jnp.stack([src, dst])
    h = jnp.maximum(_layernorm(x, axis=-1), 0.0)
    x = x + _L0_gnn_ref(h, edge_index, L0_gnn_W1, L0_gnn_a_src1, L0_gnn_a_dst1, L0_gnn_b1, L0_gnn_W2, L0_gnn_a_src2, L0_gnn_a_dst2, L0_gnn_b2)
    h = jnp.maximum(_layernorm(x, axis=-1), 0.0)
    x = x + _L1_gnn_ref(h, edge_index, L1_gnn_Wq, L1_gnn_bq, L1_gnn_Wk, L1_gnn_bk, L1_gnn_Wv, L1_gnn_bv, L1_gnn_Wskip, L1_gnn_bskip, L1_gnn_Wo, L1_gnn_bo, L1_gnn_g1, L1_gnn_b1, L1_gnn_Wf1, L1_gnn_bf1, L1_gnn_Wf2, L1_gnn_bf2, L1_gnn_g2, L1_gnn_b2)
    h = jnp.maximum(_layernorm(x, axis=-1), 0.0)
    x = x + _L2_gnn_ref(h, edge_weight, src, dst, L2_gnn_Wm, L2_gnn_bm, L2_gnn_W1, L2_gnn_b1, L2_gnn_W2, L2_gnn_b2)
    h = jnp.maximum(_layernorm(x, axis=-1), 0.0)
    x = x + _L3_gnn_ref(h, src, dst)
    return x

_drawn_inputs = setup_inputs


def setup_inputs(seed=0):
    import zlib

    import numpy as np

    out = dict(_drawn_inputs(seed))
    spreads = {'L0_gnn_b1': (0.0, 0.1),
     'L0_gnn_b2': (0.0, 0.1),
     'L1_gnn_bq': (0.0, 2.0),
     'L1_gnn_bk': (0.0, 2.0),
     'L1_gnn_bv': (0.0, 0.394),
     'L1_gnn_bskip': (0.0, 0.402),
     'L1_gnn_bo': (0.0, 0.1),
     'L1_gnn_g1': (1.0, 0.2),
     'L1_gnn_b1': (0.0, 0.1),
     'L1_gnn_bf1': (0.0, 0.508),
     'L1_gnn_bf2': (0.0, 0.1),
     'L1_gnn_g2': (1.0, 0.2),
     'L1_gnn_b2': (0.0, 0.1)}
    factors = {'edge_weight': 8.0,
     'L0_gnn_a_dst1': 37.056,
     'L0_gnn_a_src2': 8.0,
     'L0_gnn_a_dst2': 64.0,
     'L1_gnn_Wq': 53.198,
     'L1_gnn_Wk': 46.438,
     'L2_gnn_bm': 2.886,
     'L2_gnn_b1': 2.702}
    for name, (base, spread) in spreads.items():
        noise = np.random.default_rng([zlib.crc32(name.encode()), seed]).standard_normal(out[name].shape)
        drawn = base * np.exp(spread * noise) if base else spread * noise
        out[name] = jnp.asarray(drawn.astype(out[name].dtype))
    for name, factor in factors.items():
        out[name] = (out[name] * factor).astype(out[name].dtype)
    return out
```

```python
import concourse.bass as bass
from concourse import mybir
from contextlib import ExitStack

P = 128
G = 16
GE = G * P
SLOTS = 3
QUAD = 4
QUADS = G // QUAD
NT = 125
BANK = 512
BIG = 1e30
C_IN = 128
HID = 64
ROW1 = HID + 2
HEADS = 8
HD = C_IN // HEADS
FF = 512
EPS_LN = 1e-5
EPS_SM = 1e-16
SLOPE = 0.2


def chunk_counts(E):
    groups = -(-E // GE)
    return groups * G, groups


def constants():
    import numpy as np
    p = np.arange(P)
    parts = [
        ("ident", np.eye(P)),
        ("iota", np.broadcast_to(p, (P, P))),
        ("ones", np.ones((P, P))),
        ("head_of_row", p[:, None] % HEADS == np.arange(HEADS)[None, :]),
        ("chunk_of_row", p[:, None] // HEADS == np.arange(G)[None, :]),
        ("row_of_head", np.arange(P)[:, None] == p[None, :] % HEADS),
        ("feature_of_row", p[:, None] % HEADS == p[None, :] % HEADS),
    ]
    where, at = {}, 0
    for name, a in parts:
        where[name] = (at, a.shape[1])
        at += a.shape[1]
    return np.concatenate([a.astype(np.float32) for _, a in parts], 1), where


def build(nc, t, out):
    fp32, i32 = mybir.dt.float32, mybir.dt.int32
    ALU, ACT, AX = mybir.AluOpType, mybir.ActivationFunctionType, mybir.AxisListType
    DVE_ONLY, SP_ONLY = (mybir.EngineType.DVE,), (mybir.EngineType.SP,)
    ds = bass.ds

    N = t["x"].shape[0]
    E = t["src"].shape[0]
    NCH, NG = chunk_counts(E)
    EP = NCH * P
    NW = N + P
    assert NG >= 2 * SLOTS
    _, CONST = constants()

    phases = [0]

    retired = []

    class Phase(ExitStack):

        def __init__(self):
            super().__init__()
            phases[0] += 1
            self.number = phases[0]
            self.semaphores = []

        def __exit__(self, *exc):
            done = super().__exit__(*exc)
            for semaphore in self.semaphores:
                nc.gpsimd.sem_clear(semaphore)
            for semaphore in retired:
                nc.release_semaphore(semaphore)
            retired[:] = self.semaphores
            return done

    whole = Phase()

    def dram(name, shape, dt=fp32):
        return nc.dram_tensor(name, shape, dt, kind="Internal").ap()

    def sbuf(ctx, name, shape, dt=fp32):
        return ctx.enter_context(nc.sbuf_tensor(f"{name}_{ctx.number}", list(shape), dt))

    def psum(ctx, name, shape):
        return ctx.enter_context(nc.psum_tensor(f"{name}_{ctx.number}", list(shape), fp32))

    def sem(ctx, name):
        ctx.semaphores.append(nc.alloc_semaphore(f"{name}_{ctx.number}"))
        return ctx.semaphores[-1]

    def wait(eng, semaphore, value):
        if not isinstance(value, int) or value > 0:
            eng.wait_ge(semaphore, value)

    def wait_apart(eng, semaphore, value, past):
        if not isinstance(value, int):
            value = eng.to_reg(value)
        eng.wait_ge(*past)
        wait(eng, semaphore, value)

    def spread(ap, *dims):
        return bass.AP(ap.tensor, ap.offset, [list(ap.ap[0]), *[list(d) for d in dims]])

    def over_partitions(ap, n):
        return bass.AP(ap.tensor, ap.offset, [[0, n], *[list(d) for d in ap.ap]])

    def groups_loop(eng, body):
        turns = (NG - SLOTS - 1) // SLOTS
        for g in range(SLOTS):
            body(g, g)
        with eng.Fori(0, turns) as i:
            for slot in range(SLOTS):
                body(i * SLOTS + (SLOTS + slot), slot)
        for g in range(SLOTS * (turns + 1), NG):
            body(g, g % SLOTS)

    def turns_loop(eng, turns, body):
        body(0)
        if turns > 2:
            with eng.Fori(1, turns - 1) as i:
                body(i)
        if turns > 1:
            body(turns - 1)

    class Chain:

        def __init__(self, eng, semaphore, past=None):
            self.eng, self.semaphore, self.per_turn, self.past = eng, semaphore, 0, past

        def turn(self, i):
            self.i, self.at = i, 0

        def link(self, instruction, apart=False):
            self.at += 1
            if isinstance(self.i, int) and self.i == 0:
                self.per_turn = self.at
            instruction.then_inc(self.semaphore, 1)
            if apart:
                wait_apart(self.eng, self.semaphore, self.i * self.per_turn + self.at, self.past)
            else:
                self.eng.wait_ge(self.semaphore, self.i * self.per_turn + self.at)

    def uses(g, slot):
        return g // SLOTS if isinstance(g, int) else (g - slot) // SLOTS

    dst_row = dram("dst_row", (EP + 2,), i32)
    src_row = dram("src_row", (EP,), i32)
    weight_row = dram("weight_row", (EP,))
    src_idx = dram("src_idx", (NG, P, G), i32)
    dst_local = dram("dst_local", (P, NCH))
    last_local = dram("last_local", (P, NCH))
    win_base = dram("win_base", (NCH,), i32)
    seg_start = dram("seg_start", (NCH, HEADS, P))
    seg_end = dram("seg_end", (NCH, HEADS, P))
    start_row = dram("start_row", (EP,))
    one_seg = dram("one_seg", (NCH,))
    table1 = dram("table1", (N, ROW1))
    x1 = dram("x1", (N, C_IN))
    x2 = dram("x2", (N, C_IN))
    x3 = dram("x3", (N, C_IN))
    h1_T = dram("h1_T", (C_IN, N))
    q_rows = dram("q_rows", (NW, C_IN))
    kv_rows = dram("kv_rows", (N, 2 * C_IN))
    h2_T = dram("h2_T", (C_IN, N))
    zs_rows = dram("zs_rows", (N, C_IN))
    h3_rows = dram("h3_rows", (N, C_IN))

    consts = sbuf(whole, "consts", [P, t["consts"].shape[1]])
    acc = sbuf(whole, "acc", [P, 2, NW])

    def const(name, rows=P, cols=None):
        at, n = CONST[name]
        return consts[0:rows, at:at + (cols or n)]

    ident, iota, ones = const("ident"), const("iota"), const("ones")

    def prepare():
        with Phase() as ctx:
            npad = EP - E
            guard = sbuf(ctx, "guard", [1, 2], i32)
            pad_dst = sbuf(ctx, "pad_dst", [1, npad], i32)
            pad_src = sbuf(ctx, "pad_src", [1, npad], i32)
            pad_weight = sbuf(ctx, "pad_weight", [1, npad])
            zero_rows = sbuf(ctx, "zero_rows", [P, C_IN])
            raw = sbuf(ctx, "raw", [P, 4, P], i32)
            flt = sbuf(ctx, "flt", [P, 4, P])
            start = sbuf(ctx, "start", [P, P])
            end = sbuf(ctx, "end", [P, P])
            whole_c = sbuf(ctx, "whole_c", [P, 1])
            loc = sbuf(ctx, "loc", [P, P])
            is_last = sbuf(ctx, "is_last", [P, P])
            lastl = sbuf(ctx, "lastl", [P, P])
            idx_out = sbuf(ctx, "idx_out", [P, P], i32)
            loc_out = sbuf(ctx, "loc_out", [P, 2, P])
            turned = psum(ctx, "turned", [P, 3, P])
            consts_in, pads_set = sem(ctx, "consts_in"), sem(ctx, "pads_set")
            rows_padded, raw_in = sem(ctx, "rows_padded"), sem(ctx, "raw_in")
            step = sem(ctx, "step")
            turned_ready, turned_copied = sem(ctx, "turned_ready"), sem(ctx, "turned_copied")
            stored = sem(ctx, "stored")
            tiles = NCH // P
            LOADS, STORES, STEPS = 4, 8, 9
            with nc.Block() as block:
                @block.sync
                def _(sp):
                    sp.dma_start(consts[:], t["consts"]).then_inc(consts_in, 16)
                    sp.dma_start(dst_row[1:1 + E], t["dst"]).then_inc(rows_padded, 16)
                    sp.dma_start(src_row[0:E], t["src"]).then_inc(rows_padded, 16)
                    sp.dma_start(weight_row[0:E], t["edge_weight"]).then_inc(rows_padded, 16)
                    sp.wait_ge(pads_set, 6)
                    row = lambda ap: ap.rearrange("(a n) -> a n", a=1)
                    sp.dma_start(row(dst_row[0:1]), guard[0:1, 0:1]).then_inc(rows_padded, 16)
                    sp.dma_start(row(dst_row[EP + 1:EP + 2]), guard[0:1, 1:2]).then_inc(rows_padded, 16)
                    sp.dma_start(row(dst_row[1 + E:1 + EP]), pad_dst[:]).then_inc(rows_padded, 16)
                    sp.dma_start(row(src_row[E:EP]), pad_src[:]).then_inc(rows_padded, 16)
                    sp.dma_start(row(weight_row[E:EP]), pad_weight[:]).then_inc(rows_padded, 16)
                    sp.dma_start(q_rows[N:NW, :], zero_rows[:]).then_inc(stored, 16)
                    sp.wait_ge(rows_padded, 128)
                    chunk_rows = lambda ap, i: ap[ds(i * (P * P), P * P)].rearrange("(c e) -> c e", e=P)
                    with sp.Fori(0, tiles) as i:
                        sp.wait_ge(stored, i * (16 * STORES) + 16)
                        sp.wait_ge(rows_padded, 128)
                        sp.dma_start(raw[:, 0, :], chunk_rows(dst_row[1:1 + EP], i)).then_inc(raw_in, 16)
                        sp.dma_start(raw[:, 1, :], chunk_rows(dst_row[0:EP], i)).then_inc(raw_in, 16)
                        sp.dma_start(raw[:, 2, :], chunk_rows(dst_row[2:2 + EP], i)).then_inc(raw_in, 16)
                        sp.dma_start(raw[:, 3, :], chunk_rows(src_row, i)).then_inc(raw_in, 16)
                        sp.wait_ge(step, i * STEPS + STEPS)
                        sp.wait_ge(rows_padded, 128)
                        sp.dma_start(seg_start[ds(i * P, P), :, :], spread(start[:], [0, HEADS], [1, P])).then_inc(stored, 16)
                        sp.dma_start(seg_end[ds(i * P, P), :, :], spread(end[:], [0, HEADS], [1, P])).then_inc(stored, 16)
                        sp.dma_start(chunk_rows(start_row, i), start[:]).then_inc(stored, 16)
                        sp.dma_start(one_seg[ds(i * P, P)].rearrange("(c a) -> c a", a=1), whole_c[:]).then_inc(stored, 16)
                        sp.dma_start(win_base[ds(i * P, P)].rearrange("(c a) -> c a", a=1), raw[:, 0, 0:1]).then_inc(stored, 16)
                        sp.dma_start(src_idx[ds(i * (P // G), P // G), :, :].rearrange("g e c -> e g c"),
                                     idx_out[:].rearrange("e (g c) -> e g c", c=G)).then_inc(stored, 16)
                        sp.dma_start(dst_local[:, ds(i * P, P)], loc_out[:, 0, :]).then_inc(stored, 16)
                        sp.dma_start(last_local[:, ds(i * P, P)], loc_out[:, 1, :]).then_inc(stored, 16)
                    sp.wait_ge(stored, 16 * STORES * tiles + 16)

                @block.vector
                def _(dve):
                    nc.vector.memset(guard[0:1, 0:1], -1).then_inc(pads_set, 1)
                    nc.vector.memset(guard[0:1, 1:2], N + 1).then_inc(pads_set, 1)
                    nc.vector.memset(pad_dst[:], N).then_inc(pads_set, 1)
                    nc.vector.memset(pad_src[:], 0).then_inc(pads_set, 1)
                    nc.vector.memset(pad_weight[:], 0.0).then_inc(pads_set, 1)
                    nc.vector.memset(zero_rows[:], 0.0).then_inc(pads_set, 1)
                    nc.vector.memset(end[:, P - 1:P], -BIG)
                    with dve.Fori(0, tiles) as i:
                        at = [0]

                        def link(instruction):
                            at[0] += 1
                            instruction.then_inc(step, 1)
                            dve.wait_ge(step, i * STEPS + at[0])

                        dve.wait_ge(raw_in, (i + 1) * (16 * LOADS))
                        dve.wait_ge(stored, i * (16 * STORES) + 16)
                        link(nc.vector.tensor_copy(flt[:], raw[:]))
                        cur, prev, nxt = (flt[:, n, :] for n in range(3))
                        link(nc.vector.tensor_tensor(start[:], cur, prev, ALU.is_equal))
                        link(nc.vector.tensor_scalar(start[:], start[:], -1.0, BIG, ALU.add, ALU.mult))
                        nc.vector.tensor_copy(end[:, 0:P - 1], start[:, 1:P])
                        nc.vector.tensor_reduce(whole_c[:], start[:], axis=AX.X, op=ALU.min)
                        link(nc.vector.tensor_scalar(loc[:], cur, cur[:, 0:1], None, ALU.subtract))
                        link(nc.vector.tensor_tensor(is_last[:], cur, nxt, ALU.not_equal))
                        link(nc.vector.scalar_tensor_tensor(lastl[:], loc[:], 1.0, is_last[:], ALU.add, ALU.mult))
                        link(nc.vector.tensor_scalar(lastl[:], lastl[:], -1.0, None, ALU.add))
                        dve.wait_ge(turned_ready, i + 1)
                        link(nc.vector.tensor_copy(idx_out[:], turned[:, 0, :]))
                        link(nc.vector.tensor_copy(loc_out[:], turned[:, 1:3, :]))
                        assert at[0] == STEPS

                @block.tensor
                def _(pe):
                    pe.wait_ge(consts_in, 16)
                    with pe.Fori(0, tiles) as i:
                        pe.wait_ge(step, i * STEPS + (STEPS - 2))
                        nc.tensor.transpose(turned[:, 0, :], flt[:, 3, :], ident)
                        nc.tensor.transpose(turned[:, 1, :], loc[:], ident)
                        nc.tensor.transpose(turned[:, 2, :], lastl[:], ident).then_inc(turned_ready, 1)

    def turns_of(S):
        assert N % (NT * S) == 0
        return N // (NT * S)

    def node_rows(table, b):
        return table[ds(b * NT, NT), :]

    class Norm:

        def __init__(self, ctx, name, s):
            self.stats = sbuf(ctx, f"{name}_stats{s}", [NT, 6])
            self.mean_var = sbuf(ctx, f"{name}_mean_var{s}", [NT, 2])
            self.std = sbuf(ctx, f"{name}_std{s}", [NT, 1])
            self.rstd = sbuf(ctx, f"{name}_rstd{s}", [NT, 1])

        def statistics(self, chain, x):
            chain.link(nc.vector.bn_stats(self.stats[:], x), apart=True)
            return nc.vector.bn_aggr(self.mean_var[:], self.stats[:])

        def root(self, eps):
            return nc.scalar.activation(self.std[:], self.mean_var[:, 1:2], ACT.Sqrt, bias=eps)

        def scale(self, chain, y, x):
            chain.link(nc.vector.reciprocal(self.rstd[:], self.std[:]))
            return nc.vector.tensor_scalar(y, x, self.mean_var[:, 0:1], self.rstd[:], ALU.subtract, ALU.mult)

    def gat_weights(ctx, w, a_src, a_dst, k_in, k_out):
        return dict(
            w=sbuf(ctx, "w", [k_in, k_out]), w_T=sbuf(ctx, "w_T", [k_out, k_in]),
            a=sbuf(ctx, "a", [k_out, 2]), w_T_ps=psum(ctx, "w_T_ps", [k_out, k_in]),
            wa_ps=psum(ctx, "wa_ps", [k_in, 2]), to_dst=sbuf(ctx, "to_dst", [k_in, P]),
            to_src=sbuf(ctx, "to_src", [k_in, k_out + 1]), loads=((w, a_src, a_dst)))

    def nodes_first():
        S = 5
        TURNS = turns_of(S)
        with Phase() as ctx:
            W = gat_weights(ctx, t["L0_gnn_W1"], t["L0_gnn_a_src1"], t["L0_gnn_a_dst1"], C_IN, HID)
            eps = sbuf(ctx, "eps", [NT, 1])
            x = [sbuf(ctx, f"x{s}", [NT, C_IN]) for s in range(S)]
            y = [sbuf(ctx, f"y{s}", [NT, C_IN]) for s in range(S)]
            norm = [Norm(ctx, "norm", s) for s in range(S)]
            h_T = [sbuf(ctx, f"h_T{s}", [C_IN, NT]) for s in range(S)]
            rows = [sbuf(ctx, f"rows{s}", [NT, ROW1]) for s in range(S)]
            bank = [psum(ctx, f"bank{s}", [P, BANK]) for s in range(S)]
            h_T_ps = [bank[s][:, 0:NT] for s in range(S)]
            dst_ps = [bank[s][:, NT:2 * NT] for s in range(S)]
            rows_ps = [bank[s][0:NT, 2 * NT:2 * NT + HID + 1] for s in range(S)]
            weights_in, w_turned, w_T_copied = (sem(ctx, n) for n in ("weights_in", "w_turned", "w_T_copied"))
            wa_ready, weights_ready, steps = (sem(ctx, n) for n in ("wa_ready", "weights_ready", "steps"))
            x_in = [sem(ctx, f"x_in{s}") for s in range(S)]
            stored = [sem(ctx, f"stored{s}") for s in range(S)]
            var_ready, std_ready, y_ready, h_T_turned, h_T_ready, products, rows_ready = (
                sem(ctx, n) for n in ("var_ready", "std_ready", "y_ready", "h_T_turned", "h_T_ready",
                                      "products", "rows_ready"))
            with nc.Block() as block:
                @block.sync
                def _(sp):
                    sp.dma_start(W["w"][:], t["L0_gnn_W1"]).then_inc(weights_in, 16)
                    sp.dma_start(W["a"][:, 0:1], t["L0_gnn_a_src1"].rearrange("(k a) -> k a", a=1)).then_inc(weights_in, 16)
                    sp.dma_start(W["a"][:, 1:2], t["L0_gnn_a_dst1"].rearrange("(k a) -> k a", a=1)).then_inc(weights_in, 16)

                    load_x = lambda b, s: sp.dma_start(x[s][:], node_rows(t["x"], b)).then_inc(x_in[s], 16)
                    for s in range(S):
                        load_x(s, s)

                    def turn(i):
                        for s in range(S):
                            if not (isinstance(i, int) and i == TURNS - 1):
                                wait_apart(sp, y_ready, i * S + s + 1, (weights_in, 48))
                                load_x(i * S + s + S, s)
                        for s in range(S):
                            wait_apart(sp, rows_ready, i * S + s + 1, (weights_in, 48))
                            sp.dma_start(node_rows(table1, i * S + s), rows[s][:]).then_inc(stored[s], 16)
                    turns_loop(sp, TURNS, turn)
                    for s in range(S):
                        sp.wait_ge(stored[s], 16 * TURNS)

                @block.vector
                def _(dve):
                    chain = Chain(dve, steps, (weights_ready, 1))
                    nc.vector.memset(eps[:], EPS_LN)
                    for s in range(S):
                        nc.vector.memset(rows[s][:, HID + 1:ROW1], 1.0)
                    dve.wait_ge(w_turned, 1)
                    nc.vector.tensor_copy(W["w_T"][:], W["w_T_ps"][:]).then_inc(w_T_copied, 1)
                    dve.wait_ge(wa_ready, 1)
                    nc.vector.tensor_copy(W["to_src"][:, 0:HID], W["w"][:])
                    nc.vector.tensor_copy(W["to_src"][:, HID:HID + 1], W["wa_ps"][:, 0:1])
                    nc.vector.tensor_copy(W["to_dst"][:], spread(W["wa_ps"][:, 1:2], [0, P])).then_inc(weights_ready, 1)

                    def turn(i):
                        chain.turn(i)
                        for s in range(S):
                            dve.wait_ge(x_in[s], i * 16 + 16)
                            norm[s].statistics(chain, x[s][:]).then_inc(var_ready, 1)
                        for s in range(S):
                            dve.wait_ge(std_ready, i * S + s + 1)
                            wait(dve, h_T_turned, i * S - S + s + 1)
                            norm[s].scale(chain, y[s][:], x[s][:]).then_inc(y_ready, 1)
                    turns_loop(dve, TURNS, turn)

                @block.scalar
                def _(act):
                    act.wait_ge(weights_ready, 1)

                    def turn(i):
                        for s in range(S):
                            act.wait_ge(var_ready, i * S + s + 1)
                            norm[s].root(eps[:]).then_inc(std_ready, 1)
                        for s in range(S):
                            act.wait_ge(h_T_turned, i * S + s + 1)
                            nc.scalar.activation(h_T[s][:], h_T_ps[s], ACT.Relu).then_inc(h_T_ready, 1)
                        for s in range(S):
                            act.wait_ge(products, i * S + s + 1)
                            wait(act, stored[s], i * 16)
                            nc.scalar.activation(acc[:, 1, ds((i * S + s) * NT, NT)], dst_ps[s], ACT.Copy)
                            nc.scalar.activation(rows[s][:, 0:HID + 1], rows_ps[s], ACT.Copy).then_inc(rows_ready, 1)
                    turns_loop(act, TURNS, turn)

                @block.tensor
                def _(pe):
                    pe.wait_ge(weights_in, 48)
                    nc.tensor.transpose(W["w_T_ps"][:], W["w"][:], ident).then_inc(w_turned, 1)
                    pe.wait_ge(w_T_copied, 1)
                    nc.tensor.matmul(W["wa_ps"][:], W["w_T"][:], W["a"][:], start=True, stop=True).then_inc(wa_ready, 1)
                    pe.wait_ge(weights_ready, 1)

                    def turn(i):
                        for s in range(S):
                            pe.wait_ge(y_ready, i * S + s + 1)
                            wait(pe, rows_ready, i * S - S + s + 1)
                            nc.tensor.transpose(h_T_ps[s], y[s][:], ident[0:NT, 0:NT]).then_inc(h_T_turned, 1)
                        for s in range(S):
                            pe.wait_ge(h_T_ready, i * S + s + 1)
                            nc.tensor.matmul(rows_ps[s], h_T[s][:], W["to_src"][:], start=True, stop=True)
                            nc.tensor.matmul(dst_ps[s], W["to_dst"][:], h_T[s][:], start=True, stop=True).then_inc(products, 1)
                    turns_loop(pe, TURNS, turn)

    def nodes_second():
        S = 5
        TURNS = turns_of(S)
        with Phase() as ctx:
            W = gat_weights(ctx, t["L0_gnn_W2"], t["L0_gnn_a_src2"], t["L0_gnn_a_dst2"], HID, C_IN)
            bias = sbuf(ctx, "bias", [NT, HID])
            sums = [sbuf(ctx, f"sums{s}", [ROW1, NT]) for s in range(S)]
            rden = [sbuf(ctx, f"rden{s}", [NT, 1]) for s in range(S)]
            rows = [sbuf(ctx, f"rows{s}", [NT, ROW1]) for s in range(S)]
            h_T = [sbuf(ctx, f"h_T{s}", [HID, NT]) for s in range(S)]
            bank = [psum(ctx, f"bank{s}", [P, BANK]) for s in range(S)]
            node_ps = [bank[s][0:NT, 0:ROW1] for s in range(S)]
            h_T_ps = [bank[s][0:HID, ROW1:ROW1 + NT] for s in range(S)]
            dst_ps = [bank[s][:, ROW1 + NT:ROW1 + 2 * NT] for s in range(S)]
            src_ps = [bank[s][0:NT, ROW1 + 2 * NT:ROW1 + 2 * NT + 1] for s in range(S)]
            weights_in, w_turned, w_T_copied = (sem(ctx, n) for n in ("weights_in", "w_turned", "w_T_copied"))
            wa_ready, weights_ready, steps = (sem(ctx, n) for n in ("wa_ready", "weights_ready", "steps"))
            stored = [sem(ctx, f"stored{s}") for s in range(S)]
            sums_ready, node_ready, h_ready, h_T_turned, h_T_ready, products, rows_ready = (
                sem(ctx, n) for n in ("sums_ready", "node_ready", "h_ready", "h_T_turned", "h_T_ready",
                                      "products", "rows_ready"))
            with nc.Block() as block:
                @block.sync
                def _(sp):
                    sp.dma_start(W["w"][:], t["L0_gnn_W2"]).then_inc(weights_in, 16)
                    sp.dma_start(W["a"][:, 0:1], t["L0_gnn_a_src2"].rearrange("(k a) -> k a", a=1)).then_inc(weights_in, 16)
                    sp.dma_start(W["a"][:, 1:2], t["L0_gnn_a_dst2"].rearrange("(k a) -> k a", a=1)).then_inc(weights_in, 16)
                    sp.dma_start(bias[:], over_partitions(t["L0_gnn_b1"], NT)).then_inc(weights_in, 16)

                    def turn(i):
                        for s in range(S):
                            sp.wait_ge(rows_ready, i * S + s + 1)
                            sp.wait_ge(weights_in, 64)
                            sp.dma_start(node_rows(table1, i * S + s), rows[s][:]).then_inc(stored[s], 16)
                    turns_loop(sp, TURNS, turn)
                    for s in range(S):
                        sp.wait_ge(stored[s], 16 * TURNS)

                @block.vector
                def _(dve):
                    chain = Chain(dve, steps)
                    for s in range(S):
                        nc.vector.memset(rows[s][:, HID + 1:ROW1], 1.0)
                    dve.wait_ge(w_turned, 1)
                    nc.vector.tensor_copy(W["w_T"][:], W["w_T_ps"][:]).then_inc(w_T_copied, 1)
                    dve.wait_ge(wa_ready, 1)
                    nc.vector.tensor_copy(W["to_src"][:, 0:1], W["wa_ps"][:, 0:1])
                    nc.vector.tensor_copy(W["to_dst"][:], spread(W["wa_ps"][:, 1:2], [0, P])).then_inc(weights_ready, 1)

                    def turn(i):
                        chain.turn(i)
                        for s in range(S):
                            dve.wait_ge(node_ready, i * S + s + 1)
                            wait(dve, stored[s], i * 16)
                            h = rows[s][:, 0:HID]
                            chain.link(nc.vector.tensor_scalar(rden[s][:], node_ps[s][:, HID + 1:ROW1], EPS_SM, None, ALU.add))
                            chain.link(nc.vector.reciprocal(rden[s][:], rden[s][:]))
                            chain.link(nc.vector.scalar_tensor_tensor(
                                rows[s][:, 0:HID], node_ps[s][:, 0:HID], rden[s][:], bias[:],
                                ALU.mult, ALU.add))
                            nc.vector.tensor_scalar(h, h, 0.0, None, ALU.max).then_inc(h_ready, 1)
                    turns_loop(dve, TURNS, turn)

                @block.scalar
                def _(act):
                    act.wait_ge(weights_ready, 1)

                    def turn(i):
                        for s in range(S):
                            wait(act, node_ready, i * S - S + s + 1)
                            nc.scalar.activation(sums[s][:], acc[0:ROW1, 0, ds((i * S + s) * NT, NT)], ACT.Copy).then_inc(sums_ready, 1)
                        for s in range(S):
                            act.wait_ge(h_T_turned, i * S + s + 1)
                            nc.scalar.activation(h_T[s][:], h_T_ps[s], ACT.Copy).then_inc(h_T_ready, 1)
                        for s in range(S):
                            act.wait_ge(products, i * S + s + 1)
                            nc.scalar.activation(acc[:, 1, ds((i * S + s) * NT, NT)], dst_ps[s], ACT.Copy)
                            nc.scalar.activation(rows[s][:, HID:HID + 1], src_ps[s], ACT.Copy).then_inc(rows_ready, 1)
                    turns_loop(act, TURNS, turn)

                @block.tensor
                def _(pe):
                    pe.wait_ge(weights_in, 64)
                    nc.tensor.transpose(W["w_T_ps"][:], W["w"][:], ident[0:HID, 0:HID]).then_inc(w_turned, 1)
                    pe.wait_ge(w_T_copied, 1)
                    nc.tensor.matmul(W["wa_ps"][:], W["w_T"][:], W["a"][:], start=True, stop=True).then_inc(wa_ready, 1)
                    pe.wait_ge(weights_ready, 1)

                    def turn(i):
                        for s in range(S):
                            pe.wait_ge(sums_ready, i * S + s + 1)
                            wait(pe, rows_ready, i * S - S + s + 1)
                            nc.tensor.transpose(node_ps[s], sums[s][:], ident[0:ROW1, 0:ROW1]).then_inc(node_ready, 1)
                        for s in range(S):
                            wait_apart(pe, h_ready, i * S + s + 1, (weights_ready, 1))
                            nc.tensor.transpose(h_T_ps[s], rows[s][:, 0:HID], ident[0:NT, 0:NT]).then_inc(h_T_turned, 1)
                        for s in range(S):
                            pe.wait_ge(h_T_ready, i * S + s + 1)
                            nc.tensor.matmul(src_ps[s], h_T[s][:], W["to_src"][:, 0:1],
                                             start=True, stop=True)
                            nc.tensor.matmul(dst_ps[s], W["to_dst"][:], h_T[s][:], start=True, stop=True).then_inc(products, 1)
                    turns_loop(pe, TURNS, turn)

    def by_feature(ap):
        return ap.rearrange("(f a) -> f a", a=1)

    def head_major_to_dim_major(ap):
        return spread(ap, [1, HD], [HD, HEADS])

    def load_by_dim(load, to, ap, n):
        for d in range(HD):
            load(to[d * HEADS:(d + 1) * HEADS, :], bass.AP(ap.tensor, ap.offset + d * n, [[HD * n, HEADS], [1, n]]))

    def nodes_third():
        S = 4
        TURNS = turns_of(S)
        with Phase() as ctx:
            QKV = 3 * C_IN
            w_gat = sbuf(ctx, "w_gat", [ROW1, C_IN + 1])
            bias = sbuf(ctx, "bias", [NT, C_IN])
            w_qkv = sbuf(ctx, "w_qkv", [C_IN, QKV])
            b_qkv = sbuf(ctx, "b_qkv", [NT, QKV])
            w_v_raw = sbuf(ctx, "w_v_raw", [C_IN, C_IN])
            b_v_raw = sbuf(ctx, "b_v_raw", [NT, C_IN])
            eps = sbuf(ctx, "eps", [NT, 1])
            sums = [sbuf(ctx, f"sums{s}", [ROW1, NT]) for s in range(S)]
            rden = [sbuf(ctx, f"rden{s}", [NT, 1]) for s in range(S)]
            x = [sbuf(ctx, f"x{s}", [NT, C_IN]) for s in range(S)]
            xn = [sbuf(ctx, f"xn{s}", [NT, C_IN]) for s in range(S)]
            norm = [Norm(ctx, "norm", s) for s in range(S)]
            h = [sbuf(ctx, f"h{s}", [NT, C_IN]) for s in range(S)]
            h_T = [sbuf(ctx, f"h_T{s}", [C_IN, NT]) for s in range(S)]
            qkv = [sbuf(ctx, f"qkv{s}", [NT, QKV]) for s in range(S)]
            bank = [psum(ctx, f"bank{s}", [P, BANK]) for s in range(S)]
            conv_ps = [bank[s][0:NT, 0:C_IN + 1] for s in range(S)]
            h_T_ps = [bank[s][:, C_IN + 1:C_IN + 1 + NT] for s in range(S)]
            qkv_ps = [psum(ctx, f"qkv_ps{s}", [NT, QKV]) for s in range(S)]
            weights_in, weights_ready, steps = (sem(ctx, n) for n in ("weights_in", "weights_ready", "steps"))
            x_in = [sem(ctx, f"x_in{s}") for s in range(S)]
            stored = [sem(ctx, f"stored{s}") for s in range(S)]
            sums_ready, conv_ready, var_ready, std_ready, y_ready, h_T_turned, h_T_ready, projected, qkv_ready = (
                sem(ctx, n) for n in ("sums_ready", "conv_ready", "var_ready", "std_ready", "y_ready",
                                      "h_T_turned", "h_T_ready", "projected", "qkv_ready"))
            LOADS, STORES = 8, 4
            with nc.Block() as block:
                @block.sync
                def _(sp):
                    load = lambda to, ap: sp.dma_start(to, ap, allow_slow_non_contiguous=True).then_inc(weights_in, 16)
                    sp.wait_ge(weights_ready, 1)
                    load(w_gat[0:HID, 0:C_IN], t["L0_gnn_W2"])
                    load(bias[:], over_partitions(t["L0_gnn_b2"], NT))
                    load(w_qkv[:, 0:C_IN], t["L1_gnn_Wq"])
                    load(w_qkv[:, C_IN:2 * C_IN], t["L1_gnn_Wk"])
                    load(w_v_raw[:], t["L1_gnn_Wv"])
                    load(b_qkv[:, 0:C_IN], over_partitions(t["L1_gnn_bq"], NT))
                    load(b_qkv[:, C_IN:2 * C_IN], over_partitions(t["L1_gnn_bk"], NT))
                    load(b_v_raw[:], over_partitions(t["L1_gnn_bv"], NT))
                    load_x = lambda b, s: sp.dma_start(x[s][:], node_rows(t["x"], b)).then_inc(x_in[s], 16)
                    for s in range(S):
                        load_x(s, s)

                    def turn(i):
                        for s in range(S):
                            b = i * S + s
                            wait_apart(sp, var_ready, b + 1, (weights_ready, 1))
                            sp.dma_start(node_rows(x1, b), xn[s][:]).then_inc(stored[s], 16)
                            if not (isinstance(i, int) and i == TURNS - 1):
                                load_x(b + S, s)
                        for s in range(S):
                            wait_apart(sp, h_T_ready, i * S + s + 1, (weights_ready, 1))
                            sp.dma_start(h1_T[:, ds((i * S + s) * NT, NT)], h_T[s][:]).then_inc(stored[s], 16)
                        for s in range(S):
                            b = i * S + s
                            wait_apart(sp, qkv_ready, b + 1, (weights_ready, 1))
                            sp.dma_start(node_rows(q_rows, b), qkv[s][:, 0:C_IN]).then_inc(stored[s], 16)
                            sp.dma_start(node_rows(kv_rows, b), qkv[s][:, C_IN:QKV]).then_inc(stored[s], 16)
                    turns_loop(sp, TURNS, turn)
                    for s in range(S):
                        sp.wait_ge(stored[s], 16 * STORES * TURNS)

                @block.vector
                def _(dve):
                    chain = Chain(dve, steps, (weights_ready, 2))
                    nc.vector.memset(eps[:], EPS_LN)
                    nc.vector.memset(w_gat[:], 0.0).then_inc(weights_ready, 1)
                    dve.wait_ge(weights_ready, 1)
                    nc.vector.tensor_copy(w_gat[:, C_IN:C_IN + 1], ident[0:ROW1, ROW1 - 1:ROW1])
                    dve.wait_ge(weights_in, 16 * LOADS)
                    nc.vector.tensor_scalar(w_qkv[:, 0:C_IN], w_qkv[:, 0:C_IN], HD ** -0.5, None, ALU.mult)
                    nc.vector.tensor_scalar(b_qkv[:, 0:C_IN], b_qkv[:, 0:C_IN], HD ** -0.5, None, ALU.mult)
                    dims = lambda ap: ap.rearrange("p (d h) -> p d h", h=HEADS)
                    nc.vector.tensor_copy(dims(w_qkv[:, 2 * C_IN:QKV]), head_major_to_dim_major(w_v_raw[:]))
                    nc.vector.tensor_copy(dims(b_qkv[:, 2 * C_IN:QKV]), head_major_to_dim_major(b_v_raw[:])).then_inc(weights_ready, 1)
                    dve.wait_ge(weights_ready, 2)

                    def turn(i):
                        chain.turn(i)
                        for s in range(S):
                            dve.wait_ge(conv_ready, i * S + s + 1)
                            wait(dve, stored[s], i * (16 * STORES))
                            chain.link(nc.vector.tensor_scalar(rden[s][:], conv_ps[s][:, C_IN:C_IN + 1], EPS_SM, None, ALU.add))
                            chain.link(nc.vector.reciprocal(rden[s][:], rden[s][:]))
                            last = nc.vector.scalar_tensor_tensor(xn[s][:], conv_ps[s][:, 0:C_IN], rden[s][:],
                                                                  bias[:], ALU.mult, ALU.add)
                            chain.link(last)
                            dve.wait_ge(x_in[s], i * 16 + 16)
                            chain.link(nc.vector.tensor_tensor(xn[s][:], xn[s][:], x[s][:], ALU.add))
                            norm[s].statistics(chain, xn[s][:]).then_inc(var_ready, 1)
                        for s in range(S):
                            dve.wait_ge(std_ready, i * S + s + 1)
                            norm[s].scale(chain, h[s][:], xn[s][:]).then_inc(y_ready, 1)
                        for s in range(S):
                            dve.wait_ge(projected, i * S + s + 1)
                            nc.vector.tensor_tensor(qkv[s][:], qkv_ps[s][:], b_qkv[:], ALU.add).then_inc(qkv_ready, 1)
                    turns_loop(dve, TURNS, turn)

                @block.scalar
                def _(act):
                    act.wait_ge(weights_ready, 2)

                    def turn(i):
                        for s in range(S):
                            wait(act, conv_ready, i * S - S + s + 1)
                            nc.scalar.activation(sums[s][:], acc[0:ROW1, 0, ds((i * S + s) * NT, NT)], ACT.Copy).then_inc(sums_ready, 1)
                        for s in range(S):
                            act.wait_ge(var_ready, i * S + s + 1)
                            norm[s].root(eps[:]).then_inc(std_ready, 1)
                        for s in range(S):
                            act.wait_ge(h_T_turned, i * S + s + 1)
                            wait(act, stored[s], i * (16 * STORES))
                            nc.scalar.activation(h_T[s][:], h_T_ps[s], ACT.Relu).then_inc(h_T_ready, 1)
                    turns_loop(act, TURNS, turn)

                @block.tensor
                def _(pe):
                    pe.wait_ge(weights_ready, 2)

                    def turn(i):
                        for s in range(S):
                            pe.wait_ge(sums_ready, i * S + s + 1)
                            wait(pe, var_ready, i * S - S + s + 1)
                            nc.tensor.matmul(conv_ps[s], sums[s][:], w_gat[:], start=True, stop=True).then_inc(conv_ready, 1)
                        for s in range(S):
                            pe.wait_ge(y_ready, i * S + s + 1)
                            nc.tensor.transpose(h_T_ps[s], h[s][:], ident[0:NT, 0:NT]).then_inc(h_T_turned, 1)
                        for s in range(S):
                            pe.wait_ge(h_T_ready, i * S + s + 1)
                            wait(pe, qkv_ready, i * S - S + s + 1)
                            nc.tensor.matmul(qkv_ps[s][:], h_T[s][:], w_qkv[:], start=True, stop=True).then_inc(projected, 1)
                    turns_loop(pe, TURNS, turn)

    class Softmax:

        def __init__(self, ctx, heads, begun):
            self.heads, self.rows, self.begun = heads, heads * G, begun
            H, R = self.heads, self.rows
            self.start = [sbuf(ctx, f"start{n}", [R, P]) for n in range(SLOTS)]
            self.end = [sbuf(ctx, f"end{n}", [R, P]) for n in range(SLOTS)]
            self.one = [sbuf(ctx, f"one{n}", [H, G]) for n in range(SLOTS)]
            self.score = sbuf(ctx, "score", [P, R])
            self.run_max = sbuf(ctx, "run_max", [R, P])
            self.shift = sbuf(ctx, "shift", [R, P])
            self.last = sbuf(ctx, "last", [R, G])
            self.over_chunks = [sbuf(ctx, f"over_chunks{n}", [H, G + 1]) for n in range(SLOTS)]
            self.before = sbuf(ctx, "before", [R, 1])
            self.before_all = sbuf(ctx, "before_all", [R, G])
            self.expo = sbuf(ctx, "expo", [R, P + 1])
            self.exps = sbuf(ctx, "exps", [R, P + 1])
            self.scales = sbuf(ctx, "scales", [R, G])
            self.rescale = [sbuf(ctx, f"rescale{n}", [P, G]) for n in range(SLOTS)]
            self.turned = psum(ctx, "turned", [R, P])
            self.small = psum(ctx, "small", [P, 3 * G + R])
            if heads == 1:
                self.pick_chunk, self.pick_head = const("ident", R, G), const("ones", R, 1)
                self.pick_row, self.pick_feature = const("ones", 1, R), const("ones", R, P)
            else:
                self.pick_chunk, self.pick_head = const("chunk_of_row"), const("head_of_row")
                self.pick_row, self.pick_feature = const("row_of_head", H), const("feature_of_row")
            names = ("score_ready", "turned_ready", "last_ready", "by_head", "running", "by_row",
                     "shifted", "exps_ready", "scales_ready", "by_edge", "weights_ready")
            (self.score_ready, self.turned_ready, self.last_ready, self.by_head, self.running,
             self.by_row, self.shifted, self.exps_ready, self.scales_ready, self.by_edge,
             self.weights_ready) = (sem(ctx, n) for n in names)
            self.structure_in = [sem(ctx, f"structure_in{n}") for n in range(SLOTS)]
            self.LOADS = 3

        def load(self, sp, g, slot):
            H, mine = self.heads, self.structure_in[slot]
            wait(sp, self.shifted, g - SLOTS + 1)
            sp.wait_ge(self.begun, 1)
            per_row = lambda ap: ap[ds(g * G, G), 0:H, :].rearrange("c h e -> (c h) e")
            sp.dma_start(self.start[slot][:], per_row(seg_start)).then_inc(mine, 16)
            sp.dma_start(self.end[slot][:], per_row(seg_end)).then_inc(mine, 16)
            sp.dma_start(self.one[slot][:], over_partitions(one_seg[ds(g * G, G)], H)).then_inc(mine, 16)

        def dve_begin(self):
            return nc.vector.memset(self.over_chunks[SLOTS - 1][:, G:G + 1], -BIG)

        def dve_last(self, dve, chain, g, slot):
            dve.wait_ge(self.structure_in[slot], (uses(g, slot) + 1) * (16 * self.LOADS))
            dve.wait_ge(self.turned_ready, g + 1)
            chain.link(nc.vector.tensor_tensor_scan(self.run_max[:], self.start[slot][:], self.turned[:], -BIG, ALU.add, ALU.max))
            nc.vector.tensor_scalar(self.last[:], self.pick_chunk, self.run_max[:, P - 1:P], None, ALU.mult).then_inc(self.last_ready, 1)

        def dve_running(self, dve, chain, g, slot):
            H, before = self.heads, self.over_chunks[(slot - 1) % SLOTS]
            now = self.over_chunks[slot]
            nc.vector.tensor_copy(now[:, 0:1], before[:, G:G + 1])
            dve.wait_ge(self.by_head, g + 1)
            nc.vector.tensor_tensor_scan(now[:, 1:G + 1], self.one[slot][:], self.small[0:H, 0:G], before[:, G:G + 1], ALU.add, ALU.max).then_inc(self.running, 1)

        def dve_shift(self, dve, chain, g, slot):
            R = self.rows
            dve.wait_ge(self.by_row, g + 1)
            chain.link(nc.vector.tensor_tensor(self.before_all[:], self.small[0:R, G:2 * G], self.pick_chunk, ALU.mult))
            chain.link(nc.vector.tensor_reduce(self.before[:], self.before_all[:], axis=AX.X, op=ALU.add))
            chain.link(nc.vector.tensor_tensor_scan(self.run_max[:], self.start[slot][:], self.turned[:], self.before[:], ALU.add, ALU.max))
            back = lambda ap: spread(ap[:, P - 1:P], [-1, P])
            chain.link(nc.vector.tensor_tensor_scan(back(self.shift), back(self.end[slot]), back(self.run_max), -BIG, ALU.add, ALU.max))
            nc.vector.tensor_tensor(self.expo[:, 0:P], self.turned[:], self.shift[:], ALU.subtract)
            nc.vector.tensor_scalar(self.expo[:, P:P + 1], self.before[:], self.shift[:, 0:1], 0.0, ALU.subtract, ALU.min).then_inc(self.shifted, 1)

        def dve_scales(self, dve, g):
            dve.wait_ge(self.exps_ready, g + 1)
            nc.vector.tensor_scalar(self.scales[:], self.pick_chunk, self.exps[:, P:P + 1], None, ALU.mult).then_inc(self.scales_ready, 1)

        def pe_turn(self, pe, g):
            pe.wait_ge(self.begun, 1)
            pe.wait_ge(self.score_ready, g + 1)
            nc.tensor.transpose(self.turned[:], self.score[:], ident).then_inc(self.turned_ready, 1)

        def pe_by_head(self, pe, g):
            pe.wait_ge(self.begun, 1)
            pe.wait_ge(self.last_ready, g + 1)
            nc.tensor.matmul(self.small[0:self.heads, 0:G], self.pick_head, self.last[:], start=True, stop=True).then_inc(self.by_head, 1)

        def pe_by_row(self, pe, g, slot):
            pe.wait_ge(self.begun, 1)
            pe.wait_ge(self.running, g + 1)
            nc.tensor.matmul(self.small[0:self.rows, G:2 * G], self.pick_row, self.over_chunks[slot][:, 0:G], start=True, stop=True).then_inc(self.by_row, 1)

        def pe_by_edge(self, pe, g):
            R = self.rows
            pe.wait_ge(self.begun, 1)
            pe.wait_ge(self.exps_ready, g + 1)
            nc.tensor.transpose(self.small[:, 3 * G:3 * G + R], self.exps[:, 0:P], ident[0:R, 0:R])
            pe.wait_ge(self.begun, 1)
            pe.wait_ge(self.scales_ready, g + 1)
            nc.tensor.matmul(self.small[:, 2 * G:3 * G], self.pick_feature, self.scales[:], start=True, stop=True).then_inc(self.by_edge, 1)

        def act_exp(self, act, g):
            act.wait_ge(self.shifted, g + 1)
            nc.scalar.activation(self.exps[:], self.expo[:], ACT.Exp).then_inc(self.exps_ready, 1)

        def edge_weights(self):
            return self.small[:, 3 * G:3 * G + self.rows]

        def chunk_scales(self):
            return self.small[:, 2 * G:3 * G]

    rows_in = [[nc.alloc_semaphore(f"rows_in{n}_{j}") for j in range(QUADS)] for n in range(SLOTS)]
    passes = [-1]

    def gathered(g, slot):
        fills = len(range(slot, NG, SLOTS))
        return (uses(g, slot) + passes[0] * fills) * (16 * QUAD)

    def pool_gathers(pool, begun, idx_in, used, per_group, table, idx, rows, parts=1):
        def body(g, slot):
            pool.wait_ge(idx_in[slot], (uses(g, slot) + 1) * 16)
            for k in range(G):
                if k % (G // parts) == 0:
                    wait_apart(pool, used, (g - SLOTS) * per_group + per_group * (k * parts // G + 1) // parts, (begun, 1))
                pool.indirect_dma_start(out=rows[slot][:, k, :], out_offset=None, in_=table[:, :],
                                        in_offset=bass.IndirectOffsetOnAxis(ap=idx[slot][:, k:k + 1], axis=0)
                                        ).then_inc(rows_in[slot][k // QUAD], 16)
        groups_loop(pool, body)

    def load_bases(base, c, n, engines):
        _, values = nc.values_load_multi_w_load_instructions(
            base[0:1, ds(c, n)], engines=engines, min_val=0, max_val=N,
            skip_runtime_bounds_check_because="a dst, or N for padding")
        return values

    def edges_gat():
        with Phase() as ctx:
            passes[0] += 1
            begun = sem(ctx, "begun")
            sm = Softmax(ctx, 1, begun)
            idx = [sbuf(ctx, f"idx{n}", [P, G], i32) for n in range(SLOTS)]
            rows = [sbuf(ctx, f"rows{n}", [P, G, ROW1]) for n in range(SLOTS)]
            local = sbuf(ctx, "local", [P, NCH])
            copies = sbuf(ctx, "copies", [P, NCH])
            base = sbuf(ctx, "base", [1, NCH], i32)
            weight = [sbuf(ctx, f"weight{n}", [P, G]) for n in range(SLOTS)]
            dst_score = [sbuf(ctx, f"dst_score{n}", [P, G]) for n in range(SLOTS)]
            picked = sbuf(ctx, "picked", [P, 2, P])
            raw_score = sbuf(ctx, "raw_score", [P, G])
            minus = [sbuf(ctx, f"minus{n}", [P, G]) for n in range(SLOTS)]
            hot = [sbuf(ctx, f"hot{n}", [P, QUAD, P]) for n in range(2)]
            window = psum(ctx, "window", [P, 4, BANK])
            fixed_in, idx_in = sem(ctx, "fixed_in"), [sem(ctx, f"idx_in{n}") for n in range(SLOTS)]
            first, steps = sem(ctx, "first"), sem(ctx, "steps")
            distance, hot_ready, summed, added = (sem(ctx, n) for n in ("distance", "hot_ready", "summed", "added"))
            AFTER = {1: "score", 3: "last", 5: "running", 7: "shift", 11: "scales", 14: "weights"}
            with nc.Block() as block:
                @block.sync
                def _(sp):
                    sp.dma_start(local[:], dst_local).then_inc(fixed_in, 16)
                    sp.dma_start(copies[:], last_local).then_inc(fixed_in, 16)
                    sp.dma_start(base[:], win_base.rearrange("(a c) -> a c", a=1)).then_inc(fixed_in, 16)

                    def body(g, slot):
                        for j in range(QUADS):
                            wait(sp, rows_in[slot][j], gathered(g, slot))
                        wait(sp, begun, 1)
                        sp.dma_start(idx[slot][:], src_idx[ds(g, 1), :, :].rearrange("a e c -> (a e) c")).then_inc(idx_in[slot], 16)
                        sm.load(sp, g, slot)
                    groups_loop(sp, body)

                @block.gpsimd
                def _(pool):
                    pool_gathers(pool, begun, idx_in, summed, G, table1, idx, rows)

                @block.vector
                def _(dve):
                    chain = Chain(dve, steps)
                    sm.dve_begin().then_inc(begun, 1)
                    nc.vector.memset(acc[:, 1, N:NW], 0.0)
                    nc.vector.memset(acc[:, 0, :], 0.0)
                    dve.wait_ge(begun, 1)
                    dve.wait_ge(fixed_in, 48)
                    nc.vector.tensor_scalar(copies[:], copies[:], 0.0, 1.0, ALU.is_ge, ALU.add).then_inc(begun, 1)
                    dve.wait_ge(begun, 2)

                    def pick(c, k, slot, at):
                        return nc.vector.scalar_tensor_tensor(
                            picked[:, k % 2, :], iota, local[:, ds(c, 1)], acc[:, 1, ds(at, P)],
                            ALU.is_equal, ALU.mult, accum_out=dst_score[slot][:, k:k + 1])

                    done = [0]

                    def pick_first(c0, slot):
                        for q in range(0, G, 4):
                            at = load_bases(base, c0 + q, 4, DVE_ONLY)
                            for k in range(q, q + 4):
                                done[0] += 1
                                pick(c0 + k, k, slot, at[k - q]).then_inc(first, 1)
                                dve.wait_ge(first, done[0])

                    def add(g, slot, k, at):
                        dve.wait_ge(summed, g * G + (k + 1))
                        wait(dve, added, g * G + k)
                        win = acc[0:ROW1, 0, ds(at, P)]
                        nc.vector.scalar_tensor_tensor(win, win, sm.rescale[slot][0:ROW1, k:k + 1], window[0:ROW1, k % 4, 0:P],
                                                       ALU.mult, ALU.add).then_inc(added, 1)

                    def body(g, slot, scores=True, sums=True):
                        before, behind = (slot - 1) % SLOTS, (slot + 1) % SLOTS
                        if scores:
                            chain.turn(g)
                        for k in range(G):
                            if sums:
                                if k % 4 == 0:
                                    if k:
                                        held = at[3]
                                    at = load_bases(base, g * G + (k - G), 4, DVE_ONLY)
                            if scores and sums and not (isinstance(g, int) and g == NG - 1):
                                if k % 4 == 0:
                                    ahead = load_bases(base, g * G + (k + G), 4, DVE_ONLY)
                                pick(g * G + (k + G), k, behind, ahead[k % 4])
                            if sums and k:
                                add(g - 1, before, k - 1, at[k % 4 - 1] if k % 4 else held)
                            if scores and k in AFTER:
                                what = AFTER[k]
                                if what == "score":
                                    for j in range(QUADS):
                                        dve.wait_ge(rows_in[slot][j], gathered(g, slot) + 16 * QUAD)
                                    chain.link(nc.vector.tensor_tensor(raw_score[:], rows[slot][:, :, HID], dst_score[slot][:], ALU.add))
                                    nc.vector.scalar_tensor_tensor(sm.score[:], raw_score[:], SLOPE, raw_score[:], ALU.mult, ALU.max).then_inc(sm.score_ready, 1)
                                elif what == "last":
                                    sm.dve_last(dve, chain, g, slot)
                                elif what == "running":
                                    sm.dve_running(dve, chain, g, slot)
                                elif what == "shift":
                                    sm.dve_shift(dve, chain, g, slot)
                                elif what == "scales":
                                    sm.dve_scales(dve, g)
                                else:
                                    dve.wait_ge(sm.by_edge, g + 1)
                                    twice = copies[:, ds(g * G, G)]
                                    nc.vector.tensor_tensor(weight[slot][:], sm.edge_weights(), twice, ALU.mult)
                                    nc.vector.scalar_tensor_tensor(minus[slot][:], sm.edge_weights(), -1.0, twice, ALU.mult, ALU.mult)
                                    nc.vector.tensor_copy(sm.rescale[slot][:], sm.chunk_scales()).then_inc(sm.weights_ready, 1)
                        if sums:
                            add(g - 1, before, G - 1, at[3])

                    pick_first(0, 0)
                    pick_first(G, 1)
                    groups_loop(dve, lambda g, slot: body(g, slot, sums=not (isinstance(g, int) and g == 0)))
                    body(NG, NG % SLOTS, scores=False)

                @block.scalar
                def _(act):
                    act.wait_ge(fixed_in, 48)

                    def one_hot(g, slot, j):
                        wait(act, summed, g * G + (j - 1) * QUAD)
                        for n in range(QUAD):
                            last = nc.scalar.activation(hot[j % 2][:, n, :], iota, ACT.Abs, bias=local[:, ds(g * G + (j * QUAD + n), 1)], scale=-1.0)
                        last.then_inc(distance, 1)
                        act.wait_ge(distance, g * QUADS + (j + 1))
                        if j == 0:
                            act.wait_ge(sm.weights_ready, g + 1)
                        for n in range(QUAD):
                            k = j * QUAD + n
                            last = nc.scalar.activation(hot[j % 2][:, n, :], hot[j % 2][:, n, :], ACT.Relu,
                                                        bias=weight[slot][:, k:k + 1], scale=minus[slot][:, k:k + 1])
                        last.then_inc(hot_ready, 1)

                    def body(g, slot, scores=True, sums=True):
                        for j in range(QUADS):
                            if sums:
                                one_hot(g - 1, (slot - 1) % SLOTS, j)
                            if scores and j == 2:
                                sm.act_exp(act, g)
                    groups_loop(act, lambda g, slot: body(g, slot, sums=not (isinstance(g, int) and g == 0)))
                    body(NG, NG % SLOTS, scores=False)

                @block.tensor
                def _(pe):
                    pe.wait_ge(begun, 1)

                    def body(g, slot, scores=True, sums=True):
                        before = (slot - 1) % SLOTS
                        for k in range(G):
                            if sums:
                                if k % QUAD == 0:
                                    pe.wait_ge(hot_ready, g * QUADS + (k // QUAD - QUADS + 1))
                                wait(pe, added, g * G + (k - G - QUAD + 1))
                                nc.tensor.matmul(window[0:ROW1, k % 4, 0:P], rows[before][:, k, :], hot[k // QUAD % 2][:, k % QUAD, :],
                                                 start=True, stop=True).then_inc(summed, 1)
                            if scores and k in AFTER:
                                what = AFTER[k]
                                if what == "score":
                                    sm.pe_turn(pe, g)
                                elif what == "last":
                                    sm.pe_by_head(pe, g)
                                elif what == "running":
                                    sm.pe_by_row(pe, g, slot)
                                elif what == "scales":
                                    sm.pe_by_edge(pe, g)
                    groups_loop(pe, lambda g, slot: body(g, slot, sums=not (isinstance(g, int) and g == 0)))
                    body(NG, NG % SLOTS, scores=False)

    def edges_transformer():
        with Phase() as ctx:
            passes[0] += 1
            begun = sem(ctx, "begun")
            sm = Softmax(ctx, HEADS, begun)
            idx = [sbuf(ctx, f"idx{n}", [P, G], i32) for n in range(SLOTS)]
            rows = [sbuf(ctx, f"rows{n}", [P, G, 2 * C_IN]) for n in range(SLOTS)]
            hot = [sbuf(ctx, f"hot{n}", [P, G, P]) for n in range(SLOTS)]
            local = [sbuf(ctx, f"local{n}", [P, G]) for n in range(SLOTS)]
            weight = sbuf(ctx, "weight", [P, G, HD, HEADS])
            base = sbuf(ctx, "base", [1, NCH], i32)
            q_win = [sbuf(ctx, f"q_win{n}", [P, QUAD, C_IN]) for n in range(2)]
            hot_T = [sbuf(ctx, f"hot_T{n}", [P, QUAD, P]) for n in range(2)]
            hot_T_ps = psum(ctx, "hot_T_ps", [P, QUAD, P])
            q_edge = psum(ctx, "q_edge", [P, QUAD, C_IN])
            window = psum(ctx, "window", [P, QUAD, BANK])
            local_in = [sem(ctx, f"local_in{n}") for n in range(SLOTS)]
            fixed_in, idx_in = sem(ctx, "fixed_in"), [sem(ctx, f"idx_in{n}") for n in range(SLOTS)]
            q_win_in = [sem(ctx, f"q_win_in{n}") for n in range(2)]
            steps, distance, hot_ready, hot_T_turned, hot_T_ready, q_expanded, multiplied = (
                sem(ctx, n) for n in ("steps", "distance", "hot_ready", "hot_T_turned", "hot_T_ready",
                                      "q_expanded", "multiplied"))
            v_weighted, summed, added = (sem(ctx, n) for n in ("v_weighted", "summed", "added"))
            last_weights = sem(ctx, "last_weights")
            there = lambda g: not isinstance(g, int) or 0 <= g < NG

            def quad(g, slot, j):
                return g + j // QUADS, (slot + j // QUADS) % SLOTS, j % QUADS
            with nc.Block() as block:
                @block.sync
                def _(sp):
                    sp.dma_start(base[:], win_base.rearrange("(a c) -> a c", a=1)).then_inc(fixed_in, 16)
                    sp.wait_ge(fixed_in, 16)

                    def load_group(g, slot):
                        for j in range(QUADS):
                            wait(sp, rows_in[slot][j], gathered(g, slot))
                        sp.wait_ge(begun, 1)
                        sp.dma_start(idx[slot][:], src_idx[ds(g, 1), :, :].rearrange("a e c -> (a e) c")).then_inc(idx_in[slot], 16)
                        wait(sp, hot_ready, (g - SLOTS + 1) * QUADS)
                        sp.wait_ge(begun, 1)
                        sp.dma_start(local[slot][:], dst_local[:, ds(g * G, G)]).then_inc(local_in[slot], 16)
                        sm.load(sp, g, slot)

                    def load_q(g, j):
                        at = load_bases(base, g * G + j * QUAD, QUAD, SP_ONLY)
                        wait(sp, q_expanded, g * QUADS + (j - 1))
                        sp.wait_ge(fixed_in, 16)
                        for k in range(QUAD):
                            sp.dma_start(q_win[j % 2][:, k, :], q_rows[ds(at[k], P), :]).then_inc(q_win_in[j % 2], 16)

                    def body(g, slot):
                        load_group(g, slot)
                        if not isinstance(g, int) or g >= 1:
                            load_q(g - 1, 1)
                            load_q(g - 1, 2)
                            load_q(g - 1, 3)
                        load_q(g, 0)
                    groups_loop(sp, body)
                    for j in range(1, QUADS):
                        load_q(NG - 1, j)

                @block.gpsimd
                def _(pool):
                    pool_gathers(pool, begun, idx_in, summed, G, kv_rows, idx, rows, parts=QUADS)

                @block.vector
                def _(dve):
                    chain = Chain(dve, steps)
                    sm.dve_begin().then_inc(begun, 1)
                    nc.vector.memset(acc[:], 0.0).then_inc(begun, 1)
                    dve.wait_ge(begun, 2)
                    dve.wait_ge(fixed_in, 16)

                    def score(g, slot, j):
                        quad = slice(j * QUAD, (j + 1) * QUAD)
                        k_rows = rows[slot][:, quad, 0:C_IN]
                        dve.wait_ge(q_expanded, g * QUADS + (j + 1))
                        dve.wait_ge(rows_in[slot][j], gathered(g, slot) + 16 * QUAD)
                        nc.vector.tensor_tensor(k_rows, k_rows, q_edge[:], ALU.mult).then_inc(multiplied, 1)
                        dve.wait_ge(multiplied, g * QUADS + (j + 1))
                        out_ = sm.score[:, j * QUAD * HEADS:(j + 1) * QUAD * HEADS]
                        last = nc.vector.tensor_reduce(
                            out_.rearrange("e (c h) -> e c h", h=HEADS),
                            k_rows.rearrange("e c (h d) -> e c h d", d=HD), axis=AX.X, op=ALU.add)
                        if j == QUADS - 1:
                            last.then_inc(sm.score_ready, 1)

                    def add(g, slot, j, n, at):
                        k = j * QUAD + n
                        dve.wait_ge(summed, g * G + (k + 1))
                        wait(dve, added, g * G + k)
                        win = acc[:, :, ds(at[n], P)]
                        nc.vector.scalar_tensor_tensor(
                            win, win, sm.rescale[slot][:, k:k + 1],
                            window[:, n, 0:2 * P].rearrange("f (a n) -> f a n", a=2),
                            ALU.mult, ALU.add).then_inc(added, 1)

                    def weigh(g, slot, j):
                        v_rows = rows[slot][:, j * QUAD:(j + 1) * QUAD, C_IN:2 * C_IN].rearrange("e c (d h) -> e c d h", h=HEADS)
                        w = weight[:, j * QUAD:(j + 1) * QUAD, :, :]
                        nc.vector.tensor_tensor(v_rows, v_rows, w, ALU.mult).then_inc(v_weighted, 1)

                    def body(g, slot):
                        before = (slot - 1) % SLOTS
                        if there(g):
                            chain.turn(g)
                        for j in range(QUADS):
                            ahead, adding = quad(g, slot, j + 2), quad(g - 1, before, j - 1)
                            if there(ahead[0]):
                                score(*ahead)
                            if there(adding[0]):
                                at = load_bases(base, adding[0] * G + adding[2] * QUAD, QUAD, DVE_ONLY)
                                add(*adding, 0, at)
                                add(*adding, 1, at)
                            if there(g - 1):
                                if j == 0:
                                    dve.wait_ge(sm.weights_ready, g)
                                elif j == QUADS - 1:
                                    dve.wait_ge(last_weights, g)
                                weigh(g - 1, before, j)
                            if there(g) and j == 2:
                                sm.dve_running(dve, chain, g, slot)
                            elif there(g) and j == 3:
                                sm.dve_scales(dve, g)
                            if there(adding[0]):
                                add(*adding, 2, at)
                                add(*adding, 3, at)
                            if there(g) and j == 1:
                                sm.dve_last(dve, chain, g, slot)
                            elif there(g) and j == 2:
                                sm.dve_shift(dve, chain, g, slot)

                    score(0, 0, 0)
                    score(0, 0, 1)
                    groups_loop(dve, body)
                    body(NG, NG % SLOTS)
                    body(NG + 1, (NG + 1) % SLOTS)

                @block.scalar
                def _(act):
                    def one_hot(g, slot, j):
                        wait(act, summed, (g - SLOTS) * G + (j + 1) * QUAD)
                        if j == 0:
                            act.wait_ge(local_in[slot], (uses(g, slot) + 1) * 16)
                        quad = slice(j * QUAD, (j + 1) * QUAD)
                        for k in range(j * QUAD, (j + 1) * QUAD):
                            last = nc.scalar.activation(hot[slot][:, k, :], iota, ACT.Abs, bias=local[slot][:, k:k + 1], scale=-1.0)
                        last.then_inc(distance, 1)
                        act.wait_ge(distance, g * QUADS + (j + 1))
                        nc.scalar.activation(hot[slot][:, quad, :], hot[slot][:, quad, :], ACT.Relu, bias=1.0, scale=-1.0).then_inc(hot_ready, 1)

                    def copy_hot_T(g, j):
                        act.wait_ge(hot_T_turned, g * QUADS + (j + 1))
                        wait(act, q_expanded, g * QUADS + (j - 1))
                        nc.scalar.activation(hot_T[j % 2][:], hot_T_ps[:], ACT.Copy).then_inc(hot_T_ready, 1)

                    def copy_weights(g, slot, part):
                        chunks = slice(0, G - QUAD) if part == 0 else slice(G - QUAD, G)
                        n = chunks.stop - chunks.start
                        w = sm.edge_weights()[:, chunks.start * HEADS:chunks.stop * HEADS]
                        return nc.scalar.activation(weight[:, chunks, :, :], spread(w, [HEADS, n], [0, HD], [1, HEADS]), ACT.Copy)

                    def last_quad_weights(g, slot):
                        wait(act, summed, g * G)
                        copy_weights(g, slot, 1).then_inc(last_weights, 1)

                    for j in range(3):
                        one_hot(0, 0, j)
                        copy_hot_T(0, j)
                    one_hot(0, 0, 3)

                    def body(g, slot):
                        behind = (slot + 1) % SLOTS
                        for j in range(QUADS):
                            ahead = quad(g, slot, j + 3)
                            if there(ahead[0]):
                                copy_hot_T(ahead[0], ahead[2])
                            if j == 0 and there(g - 1):
                                last_quad_weights(g - 1, (slot - 1) % SLOTS)
                            if there(g + 1):
                                one_hot(g + 1, behind, j)
                            if j == 2:
                                sm.act_exp(act, g)
                        act.wait_ge(sm.by_edge, g + 1)
                        wait(act, summed, g * G - QUAD)
                        nc.scalar.activation(sm.rescale[slot][:], sm.chunk_scales(), ACT.Copy)
                        copy_weights(g, slot, 0).then_inc(sm.weights_ready, 1)
                    groups_loop(act, body)
                    last_quad_weights(NG - 1, (NG - 1) % SLOTS)

                @block.tensor
                def _(pe):
                    pe.wait_ge(begun, 1)

                    def turn_hot(g, slot, j):
                        wait(pe, hot_T_ready, g * QUADS + j)
                        pe.wait_ge(hot_ready, g * QUADS + (j + 1))
                        for k in range(QUAD):
                            last = nc.tensor.transpose(hot_T_ps[:, k, :], hot[slot][:, j * QUAD + k, :], ident)
                        last.then_inc(hot_T_turned, 1)

                    def expand_q(g, j):
                        pe.wait_ge(hot_T_ready, g * QUADS + (j + 1))
                        pe.wait_ge(q_win_in[j % 2], g * (16 * QUAD * QUADS // 2) + 16 * QUAD * (j // 2 + 1))
                        wait(pe, multiplied, g * QUADS + j)
                        for k in range(QUAD):
                            last = nc.tensor.matmul(q_edge[:, k, :], hot_T[j % 2][:, k, :], q_win[j % 2][:, k, :], start=True, stop=True)
                        last.then_inc(q_expanded, 1)

                    def sum_window(g, slot, j, n):
                        k = j * QUAD + n
                        pe.wait_ge(v_weighted, g * QUADS + (k // QUAD + 1))
                        wait(pe, added, g * G + (k - QUAD + 1))
                        w = weight[:, k, :, :].rearrange("e d h -> e (d h)")
                        nc.tensor.matmul(window[:, k % QUAD, 0:P], rows[slot][:, k, C_IN:2 * C_IN], hot[slot][:, k, :], start=True, stop=True)
                        nc.tensor.matmul(window[:, k % QUAD, P:2 * P], w, hot[slot][:, k, :], start=True, stop=True).then_inc(summed, 1)

                    for j in range(3):
                        turn_hot(0, 0, j)
                        expand_q(0, j)

                    def body(g, slot):
                        for j in range(QUADS):
                            ahead = quad(g, slot, j + 3)
                            behind, now = quad(g - 1, (slot - 1) % SLOTS, j - 1), quad(g - 1, (slot - 1) % SLOTS, j)
                            if there(g) and j == 2:
                                wait(pe, last_weights, g)
                                sm.pe_by_head(pe, g)
                            if there(ahead[0]):
                                turn_hot(*ahead)
                            if there(behind[0]):
                                sum_window(*behind, 2)
                                sum_window(*behind, 3)
                            if there(g) and j == 1:
                                sm.pe_turn(pe, g)
                            if there(ahead[0]):
                                expand_q(ahead[0], ahead[2])
                            if there(now[0]):
                                sum_window(*now, 0)
                                sum_window(*now, 1)
                            if there(g) and j == 2:
                                sm.pe_by_row(pe, g, slot)
                            elif there(g) and j == 3:
                                sm.pe_by_edge(pe, g)
                    groups_loop(pe, body)
                    body(NG, NG % SLOTS)
                    body(NG + 1, (NG + 1) % SLOTS)

    def nodes_fourth():
        S = 4
        TURNS = turns_of(S)
        HALVES = (range(0, S // 2), range(S // 2, S))
        first_turn = lambda i: isinstance(i, int) and i == 0

        def parts_loop(eng, part):
            def turn(i):
                part((i, 0), None if first_turn(i) else (i - 1, 1))
                part((i, 1), (i, 0))
            turn(0)
            turn(1)
            with eng.Fori(2, TURNS - 1) as i:
                turn(i)
            turn(TURNS - 1)
            part(None, (TURNS - 1, 1))
        with Phase() as ctx:
            KF = FF // P
            w_out = sbuf(ctx, "w_out", [C_IN, C_IN])
            w_out_raw, w_skip_raw, w_skip_T, w_res = (sbuf(ctx, n, [C_IN, C_IN]) for n in ("w_out_raw", "w_skip_raw", "w_skip_T", "w_res"))
            b_skip = sbuf(ctx, "b_skip", [C_IN, 1])
            w_ff1 = sbuf(ctx, "w_ff1", [C_IN, FF])
            w_ff2 = sbuf(ctx, "w_ff2", [P, KF, C_IN])
            b_ff1 = sbuf(ctx, "b_ff1", [P, KF])
            w_src = sbuf(ctx, "w_src", [C_IN, C_IN])
            b_out, b_ff2, b_res = (sbuf(ctx, n, [1, C_IN]) for n in ("b_out", "b_ff2", "b_res"))
            gain1, shift1 = (sbuf(ctx, n, [C_IN, 1]) for n in ("gain1", "shift1"))
            gain2, shift2 = (sbuf(ctx, n, [NT, C_IN]) for n in ("gain2", "shift2"))
            eps = sbuf(ctx, "eps", [NT, 1])
            tiles = lambda name, *shape: [sbuf(ctx, f"{name}{s}", list(shape)) for s in range(S)]
            h_T, den, conv = tiles("h_T", C_IN, NT), tiles("den", C_IN, NT), tiles("conv", C_IN, NT)
            n1, out2_T, hidden = tiles("n1", NT, C_IN), tiles("out2_T", C_IN, NT), tiles("hidden", P, KF, NT)
            x, xn, y = tiles("x", NT, C_IN), tiles("xn", NT, C_IN), tiles("y", NT, C_IN)
            hn_T, zs = tiles("hn_T", C_IN, NT), tiles("zs", NT, C_IN)
            norm1, norm2, norm3 = ([Norm(ctx, f"norm{n}", s) for s in range(S)] for n in (1, 2, 3))
            bank = [psum(ctx, f"bank{s}", [P, BANK]) for s in range(S)]
            r_ps = [bank[s][0:NT, 0:C_IN] for s in range(S)]
            zs_ps = [bank[s][0:NT, C_IN:2 * C_IN] for s in range(S)]
            turn_ps = [bank[s][:, 2 * C_IN:2 * C_IN + NT] for s in range(S)]
            ff_ps = [psum(ctx, f"ff_ps{s}", [P, KF, NT]) for s in range(S)]
            weights_in, eps_set, folded, folded_copied = (
                sem(ctx, n) for n in ("weights_in", "eps_set", "folded", "folded_copied"))
            steps = [[sem(ctx, f"steps{n}_{half}") for half in range(2)] for n in range(2)]
            h_in, x_in, stored = ([sem(ctx, f"{n}{s}") for s in range(S)] for n in ("h_in", "x_in", "stored"))
            (den_ready, conv_ready, projected, var1_ready, std1_ready, n1_ready, n1_turned, out2_T_ready, ff1_ready,
             hidden_ready, ff2_ready, var2_ready, std2_ready, n2_ready, x_shifted, x_scaled, x_ready, var3_ready, std3_ready, y_ready, y_turned,
             hn_T_ready, zs_ready, zs_copied) = (sem(ctx, n) for n in (
                 "den_ready", "conv_ready", "projected", "var1_ready", "std1_ready", "n1_ready", "n1_turned",
                 "out2_T_ready", "ff1_ready", "hidden_ready", "ff2_ready", "var2_ready", "std2_ready", "n2_ready", "x_shifted", "x_scaled", "x_ready",
                 "var3_ready", "std3_ready", "y_ready", "y_turned", "hn_T_ready", "zs_ready", "zs_copied"))
            LOADS, STORES = 13 + HD, 3
            with nc.Block() as block:
                @block.sync
                def _(sp):
                    load = lambda to, ap: sp.dma_start(to, ap).then_inc(weights_in, 16)
                    load(w_out_raw[:], t["L1_gnn_Wo"])
                    load(w_skip_raw[:], t["L1_gnn_Wskip"])
                    load(b_skip[:], by_feature(t["L1_gnn_bskip"]))
                    load_by_dim(load, w_out, t["L1_gnn_Wo"], C_IN)
                    load(w_ff1[:], t["L1_gnn_Wf1"])
                    load(w_ff2[:], t["L1_gnn_Wf2"].rearrange("(j k) c -> k j c", k=P))
                    sp.dma_start(b_ff1[:], t["L1_gnn_bf1"].rearrange("(j k) -> k j", k=P),
                                 allow_slow_non_contiguous=True).then_inc(weights_in, 16)
                    load(w_src[:], t["L2_gnn_Wm"][C_IN:2 * C_IN, :])
                    load(b_out[:], over_partitions(t["L1_gnn_bo"], 1))
                    load(b_ff2[:], over_partitions(t["L1_gnn_bf2"], 1))
                    load(gain1[:], by_feature(t["L1_gnn_g1"]))
                    load(shift1[:], by_feature(t["L1_gnn_b1"]))
                    load(gain2[:], over_partitions(t["L1_gnn_g2"], NT))
                    load(shift2[:], over_partitions(t["L1_gnn_b2"], NT))

                    def load_h(b, s):
                        sp.dma_start(h_T[s][:], h1_T[:, ds(b * NT, NT)]).then_inc(h_in[s], 16)

                    def load_x(b, s):
                        sp.dma_start(x[s][:], node_rows(x1, b)).then_inc(x_in[s], 16)
                    for s in range(S):
                        load_h(s, s)
                        load_x(s, s)

                    def turn(i):
                        more = not (isinstance(i, int) and i == TURNS - 1)

                        def after(semaphore, s):
                            wait_apart(sp, semaphore, i * S + s + 1, (weights_in, 16 * LOADS))
                        for s in range(S):
                            if more:
                                after(projected, s)
                                load_h(i * S + s + S, s)
                        for half in HALVES:
                            for s in half:
                                after(var3_ready, s)
                                sp.dma_start(node_rows(x2, i * S + s), xn[s][:]).then_inc(stored[s], 16)
                                if more:
                                    load_x(i * S + s + S, s)
                            for s in half:
                                after(hn_T_ready, s)
                                sp.dma_start(h2_T[:, ds((i * S + s) * NT, NT)], hn_T[s][:]).then_inc(stored[s], 16)
                            for s in half:
                                after(zs_copied, s)
                                sp.dma_start(node_rows(zs_rows, i * S + s), zs[s][:]).then_inc(stored[s], 16)
                    turns_loop(sp, TURNS, turn)
                    for s in range(S):
                        sp.wait_ge(stored[s], 16 * STORES * TURNS)

                @block.gpsimd
                def _(pool):
                    pool.wait_ge(weights_in, 16 * LOADS)

                    def new_x(i, half):
                        for s in HALVES[half]:
                            pool.wait_ge(x_in[s], i * 16 + 16)
                            nc.gpsimd.tensor_tensor(x[s][:], x[s][:], shift2[:], ALU.add).then_inc(x_shifted, 1)
                        for s in HALVES[half]:
                            pool.wait_ge(n2_ready, i * S + s + 1)
                            nc.gpsimd.tensor_tensor(xn[s][:], xn[s][:], gain2[:], ALU.mult).then_inc(x_scaled, 1)
                            pool.wait_ge(x_shifted, i * S + s + 1)
                            pool.wait_ge(x_scaled, i * S + s + 1)
                            nc.gpsimd.tensor_tensor(xn[s][:], xn[s][:], x[s][:], ALU.add).then_inc(x_ready, 1)

                    def part(first, second):
                        if second:
                            new_x(*second)
                    parts_loop(pool, part)

                @block.vector
                def _(dve):
                    nc.vector.memset(eps[:], EPS_LN).then_inc(eps_set, 1)
                    dve.wait_ge(weights_in, 16 * LOADS)
                    dve.wait_ge(folded, 1)
                    nc.vector.tensor_copy(w_skip_T[:], bank[0][:, 0:C_IN]).then_inc(folded_copied, 1)
                    dve.wait_ge(folded, 2)
                    nc.vector.tensor_copy(w_res[:], bank[0][:, C_IN:2 * C_IN])
                    nc.vector.tensor_copy(b_res[:], bank[0][0:1, 2 * C_IN:3 * C_IN]).then_inc(folded_copied, 1)

                    def denominators(i, half):
                        for s in HALVES[half]:
                            cols = ds((i * S + s) * NT, NT)
                            wait(dve, projected, i * S - S + s + 1)
                            nc.vector.tensor_scalar(den[s][:], acc[:, 1, cols], EPS_SM, None, ALU.add).then_inc(den_ready, 1)

                    def normalise(i, half, chain):
                        for s in HALVES[half]:
                            dve.wait_ge(den_ready, i * S + s + 1)
                            chain.link(nc.vector.reciprocal(den[s][:], den[s][:]))
                            nc.vector.tensor_tensor(conv[s][:], acc[:, 0, ds((i * S + s) * NT, NT)], den[s][:], ALU.mult).then_inc(conv_ready, 1)

                    def first_statistics(i, half, chain):
                        for s in HALVES[half]:
                            dve.wait_ge(projected, i * S + s + 1)
                            norm1[s].statistics(chain, r_ps[s]).then_inc(var1_ready, 1)

                    def first_scale(i, half, chain):
                        for s in HALVES[half]:
                            dve.wait_ge(std1_ready, i * S + s + 1)
                            norm1[s].scale(chain, n1[s][:], r_ps[s]).then_inc(n1_ready, 1)

                    def second_statistics(i, half, chain):
                        for s in HALVES[half]:
                            dve.wait_ge(ff2_ready, i * S + s + 1)
                            norm2[s].statistics(chain, r_ps[s]).then_inc(var2_ready, 1)

                    def second_scale(i, half, chain):
                        for s in HALVES[half]:
                            dve.wait_ge(std2_ready, i * S + s + 1)
                            wait(dve, stored[s], i * (16 * STORES))
                            norm2[s].scale(chain, xn[s][:], r_ps[s]).then_inc(n2_ready, 1)

                    def third_statistics(i, half, chain):
                        for s in HALVES[half]:
                            dve.wait_ge(x_ready, i * S + s + 1)
                            norm3[s].statistics(chain, xn[s][:]).then_inc(var3_ready, 1)

                    def last_scale(i, half, chain):
                        for s in HALVES[half]:
                            dve.wait_ge(std3_ready, i * S + s + 1)
                            norm3[s].scale(chain, y[s][:], xn[s][:]).then_inc(y_ready, 1)

                    chains = [[Chain(dve, steps[n][half], (eps_set, 1)) for half in range(2)] for n in range(2)]

                    def part(first, second):
                        if first:
                            one = chains[0][first[1]]
                            one.turn(first[0])
                            denominators(*first)
                            normalise(*first, one)
                            first_statistics(*first, one)
                        if second:
                            two = chains[1][second[1]]
                            two.turn(second[0])
                            second_statistics(*second, two)
                        if first:
                            first_scale(*first, one)
                        if second:
                            second_scale(*second, two)
                            third_statistics(*second, two)
                            last_scale(*second, two)
                    parts_loop(dve, part)

                @block.scalar
                def _(act):
                    act.wait_ge(eps_set, 1)
                    act.wait_ge(weights_in, 16 * LOADS)

                    now = lambda i, semaphore, s: act.wait_ge(semaphore, i * S + s + 1)

                    def first_root(i, half):
                        for s in HALVES[half]:
                            now(i, var1_ready, s)
                            norm1[s].root(eps[:]).then_inc(std1_ready, 1)

                    def copy_out2(i, half):
                        for s in HALVES[half]:
                            now(i, n1_turned, s)
                            nc.scalar.activation(out2_T[s][:], turn_ps[s], ACT.Identity, bias=shift1[:], scale=gain1[:]).then_inc(out2_T_ready, 1)

                    def copy_hidden(i, half):
                        for s in HALVES[half]:
                            now(i, ff1_ready, s)
                            for j in range(KF):
                                last = nc.scalar.activation(hidden[s][:, j, :], ff_ps[s][:, j, :], ACT.Relu, bias=b_ff1[:, j:j + 1])
                            last.then_inc(hidden_ready, 1)

                    def second_root(i, half):
                        for s in HALVES[half]:
                            now(i, var2_ready, s)
                            norm2[s].root(eps[:]).then_inc(std2_ready, 1)

                    def third_root(i, half):
                        for s in HALVES[half]:
                            now(i, var3_ready, s)
                            norm3[s].root(eps[:]).then_inc(std3_ready, 1)

                    def copy_h2(i, half):
                        for s in HALVES[half]:
                            now(i, y_turned, s)
                            wait(act, stored[s], i * (16 * STORES))
                            nc.scalar.activation(hn_T[s][:], turn_ps[s], ACT.Relu).then_inc(hn_T_ready, 1)

                    def copy_zs(i, half):
                        for s in HALVES[half]:
                            now(i, zs_ready, s)
                            nc.scalar.activation(zs[s][:], zs_ps[s], ACT.Copy).then_inc(zs_copied, 1)

                    def part(first, second):
                        if first:
                            first_root(*first)
                        if second:
                            second_root(*second)
                        if first:
                            copy_out2(*first)
                        if second:
                            third_root(*second)
                        if first:
                            copy_hidden(*first)
                        if second:
                            copy_h2(*second)
                            copy_zs(*second)
                    parts_loop(act, part)

                @block.tensor
                def _(pe):
                    pe.wait_ge(weights_in, 16 * LOADS)
                    nc.tensor.transpose(bank[0][:, 0:C_IN], w_skip_raw[:], ident).then_inc(folded, 1)
                    pe.wait_ge(folded_copied, 1)
                    nc.tensor.matmul(bank[0][:, C_IN:2 * C_IN], w_skip_T[:], w_out_raw[:], start=True, stop=False)
                    nc.tensor.matmul(bank[0][:, C_IN:2 * C_IN], ident, ident, start=False, stop=True)
                    nc.tensor.matmul(bank[0][0:1, 2 * C_IN:3 * C_IN], b_skip[:], w_out_raw[:], start=True, stop=False)
                    nc.tensor.matmul(bank[0][0:1, 2 * C_IN:3 * C_IN], ones[0:1, 0:1], b_out[:], start=False, stop=True).then_inc(folded, 1)
                    pe.wait_ge(folded_copied, 2)
                    one_row = ones[0:1, 0:NT]

                    now = lambda i, semaphore, s: pe.wait_ge(semaphore, i * S + s + 1)

                    def project(i, half):
                        for s in HALVES[half]:
                            now(i, conv_ready, s)
                            pe.wait_ge(h_in[s], i * 16 + 16)
                            wait(pe, zs_copied, i * S - S + s + 1)
                            nc.tensor.matmul(r_ps[s], conv[s][:], w_out[:], start=True, stop=False)
                            nc.tensor.matmul(r_ps[s], h_T[s][:], w_res[:], start=False, stop=False)
                            nc.tensor.matmul(r_ps[s], one_row, b_res[:], start=False, stop=True).then_inc(projected, 1)

                    def turn_n1(i, half):
                        for s in HALVES[half]:
                            now(i, n1_ready, s)
                            nc.tensor.transpose(turn_ps[s], n1[s][:], ident[0:NT, 0:NT]).then_inc(n1_turned, 1)

                    def feed_forward1(i, half):
                        for s in HALVES[half]:
                            now(i, out2_T_ready, s)
                            wait(pe, hidden_ready, i * S - S + s + 1)
                            for j in range(KF):
                                last = nc.tensor.matmul(ff_ps[s][:, j, :], w_ff1[:, j * P:(j + 1) * P], out2_T[s][:], start=True, stop=True)
                            last.then_inc(ff1_ready, 1)

                    def feed_forward2(i, half):
                        for s in HALVES[half]:
                            now(i, hidden_ready, s)
                            nc.tensor.matmul(r_ps[s], out2_T[s][:], ident, start=True, stop=False)
                            for j in range(KF):
                                nc.tensor.matmul(r_ps[s], hidden[s][:, j, :], w_ff2[:, j, :], start=False, stop=False)
                            nc.tensor.matmul(r_ps[s], one_row, b_ff2[:], start=False, stop=True).then_inc(ff2_ready, 1)

                    def turn_y(i, half):
                        for s in HALVES[half]:
                            now(i, y_ready, s)
                            nc.tensor.transpose(turn_ps[s], y[s][:], ident[0:NT, 0:NT]).then_inc(y_turned, 1)

                    def times_w_src(i, half):
                        for s in HALVES[half]:
                            now(i, hn_T_ready, s)
                            nc.tensor.matmul(zs_ps[s], hn_T[s][:], w_src[:], start=True, stop=True).then_inc(zs_ready, 1)

                    def part(first, second):
                        if first:
                            project(*first)
                            turn_n1(*first)
                            feed_forward1(*first)
                        if second:
                            turn_y(*second)
                        if first:
                            feed_forward2(*first)
                        if second:
                            times_w_src(*second)
                    parts_loop(pe, part)

    def load_edges(sp, g, slot, idx, idx_in, local, local_from, local_in, one_hots):
        for j in range(QUADS):
            wait(sp, rows_in[slot][j], gathered(g, slot))
        sp.dma_start(idx[slot][:], src_idx[ds(g, 1), :, :].rearrange("a e c -> (a e) c")).then_inc(idx_in[slot], 16)
        wait(sp, one_hots, (g - SLOTS + 1) * QUADS)
        sp.dma_start(local[slot][:], local_from[:, ds(g * G, G)]).then_inc(local_in[slot], 16)

    def one_hots(out_, at):
        return nc.vector.tensor_tensor(out_, spread(iota, [0, QUAD], [1, P]), spread(at, [1, QUAD], [0, P]), ALU.is_equal)

    def edges_max():
        with Phase() as ctx:
            passes[0] += 1
            begun = sem(ctx, "begun")
            idx = [sbuf(ctx, f"idx{n}", [P, G], i32) for n in range(SLOTS)]
            rows = [sbuf(ctx, f"rows{n}", [P, G, C_IN]) for n in range(SLOTS)]
            last_at = [sbuf(ctx, f"last_at{n}", [P, G]) for n in range(SLOTS)]
            start = [sbuf(ctx, f"start{n}", [P, GE]) for n in range(SLOTS)]
            edge_w = [sbuf(ctx, f"edge_w{n}", [1, GE]) for n in range(SLOTS)]
            w_edge = sbuf(ctx, "w_edge", [1, C_IN])
            base = sbuf(ctx, "base", [1, NCH], i32)
            run_max = [sbuf(ctx, f"run_max{n}", [C_IN, QUAD * P]) for n in range(2)]
            max_rows = [sbuf(ctx, f"max_rows{n}", [P, QUAD, C_IN]) for n in range(2)]
            hot = [sbuf(ctx, f"hot{n}", [P, QUAD, P]) for n in range(2)]
            message = [psum(ctx, f"message{n}", [C_IN, QUAD * P]) for n in range(2)]
            turned = [psum(ctx, f"turned{n}", [P, QUAD, C_IN]) for n in range(2)]
            window = psum(ctx, "window", [C_IN, QUAD, BANK])
            fixed_in = sem(ctx, "fixed_in")
            idx_in, local_in, start_in = ([sem(ctx, f"{n}{m}") for m in range(SLOTS)] for n in ("idx_in", "local_in", "start_in"))
            messages, scanned, turned_ready, max_ready, hot_ready, summed, added = (
                sem(ctx, n) for n in ("messages", "scanned", "turned_ready", "max_ready", "hot_ready", "summed", "added"))

            def steps(eng, step):
                def quad(g, slot, j):
                    return (g, slot, j) if j >= 0 else (g - 1, (slot - 1) % SLOTS, j + QUADS)

                def body(g, slot):
                    for j in range(QUADS):
                        there = lambda back: not isinstance(g, int) or 0 <= g * QUADS + j - back < NG * QUADS
                        if not isinstance(g, int) or g * QUADS + j < NG * QUADS + 2:
                            step(*(quad(g, slot, j - back) if there(back) else None for back in range(3)))
                groups_loop(eng, body)
                body(NG, NG % SLOTS)
            with nc.Block() as block:
                @block.sync
                def _(sp):
                    sp.dma_start(base[:], win_base.rearrange("(a c) -> a c", a=1)).then_inc(fixed_in, 16)
                    sp.dma_start(w_edge[:], t["L2_gnn_Wm"][2 * C_IN:2 * C_IN + 1, :]).then_inc(fixed_in, 16)

                    def body(g, slot):
                        load_edges(sp, g, slot, idx, idx_in, last_at, last_local, local_in, hot_ready)
                        wait(sp, scanned, (g - SLOTS + 1) * QUADS)
                        edges = ds(g * GE, GE)
                        sp.dma_start(start[slot][:], over_partitions(start_row[edges], P)).then_inc(start_in[slot], 16)
                        sp.dma_start(edge_w[slot][:], over_partitions(weight_row[edges], 1)).then_inc(start_in[slot], 16)
                    groups_loop(sp, body)

                @block.gpsimd
                def _(pool):
                    pool_gathers(pool, begun, idx_in, messages, QUADS, zs_rows, idx, rows)

                @block.vector
                def _(dve):
                    nc.vector.memset(run_max[1][:, QUAD * P - 1:QUAD * P], -BIG).then_inc(begun, 1)
                    nc.vector.memset(acc[:, 0, :], 0.0).then_inc(begun, 1)
                    dve.wait_ge(begun, 2)
                    dve.wait_ge(fixed_in, 32)

                    def step(now, one_back, two_back):
                        if now:
                            g, slot, j = now
                            if j == 0:
                                dve.wait_ge(start_in[slot], (uses(g, slot) + 1) * 32)
                            dve.wait_ge(messages, g * QUADS + (j + 1))
                            wait(dve, turned_ready, g * QUADS + (j - 1))
                            wait(dve, scanned, g * QUADS + j)
                            nc.vector.tensor_tensor_scan(
                                run_max[j % 2][:], start[slot][:, j * QUAD * P:(j + 1) * QUAD * P], message[j % 2][:],
                                run_max[(j + 1) % 2][:, QUAD * P - 1:QUAD * P], ALU.add, ALU.max).then_inc(scanned, 1)
                        if one_back:
                            g, slot, j = one_back
                            if j == 0:
                                dve.wait_ge(local_in[slot], (uses(g, slot) + 1) * 16)
                            wait(dve, summed, (g * QUADS + (j - 1)) * QUAD)
                            one_hots(hot[j % 2][:], last_at[slot][:, j * QUAD:(j + 1) * QUAD]).then_inc(hot_ready, 1)
                        if two_back:
                            g, slot, j = two_back
                            at = load_bases(base, g * G + j * QUAD, QUAD, DVE_ONLY)
                            for k in range(QUAD):
                                dve.wait_ge(summed, g * G + (j * QUAD + k + 1))
                                wait(dve, added, g * G + (j * QUAD + k))
                                win = acc[:, 0, ds(at[k], P)]
                                nc.vector.tensor_tensor(win, win, window[:, k, 0:P], ALU.add).then_inc(added, 1)
                    steps(dve, step)

                @block.scalar
                def _(act):
                    def step(now, one_back, two_back):
                        if one_back:
                            g, slot, j = one_back
                            act.wait_ge(turned_ready, g * QUADS + (j + 1))
                            wait(act, summed, (g * QUADS + (j - 1)) * QUAD)
                            nc.scalar.activation(max_rows[j % 2][:], turned[j % 2][:], ACT.Copy).then_inc(max_ready, 1)
                    steps(act, step)

                @block.tensor
                def _(pe):
                    pe.wait_ge(begun, 1)
                    pe.wait_ge(fixed_in, 32)

                    def step(now, one_back, two_back):
                        if now:
                            g, slot, j = now
                            if j == 0:
                                pe.wait_ge(start_in[slot], (uses(g, slot) + 1) * 32)
                            pe.wait_ge(begun, 1)
                            wait(pe, scanned, g * QUADS + (j - 1))
                            nc.tensor.matmul(message[j % 2][:], w_edge[:], edge_w[slot][:, j * QUAD * P:(j + 1) * QUAD * P], start=True, stop=False)
                            pe.wait_ge(rows_in[slot][j], gathered(g, slot) + 16 * QUAD)
                            for k in range(QUAD):
                                last = nc.tensor.matmul(message[j % 2][:, k * P:(k + 1) * P], rows[slot][:, j * QUAD + k, :], ident,
                                                        start=False, stop=k == QUAD - 1)
                            last.then_inc(messages, 1)
                        if one_back:
                            g, slot, j = one_back
                            wait(pe, max_ready, g * QUADS + (j - 1))
                            pe.wait_ge(scanned, g * QUADS + (j + 1))
                            for k in range(QUAD):
                                last = nc.tensor.transpose(turned[j % 2][:, k, :], run_max[j % 2][:, k * P:(k + 1) * P], ident)
                            last.then_inc(turned_ready, 1)
                        if two_back:
                            g, slot, j = two_back
                            pe.wait_ge(max_ready, g * QUADS + (j + 1))
                            pe.wait_ge(hot_ready, g * QUADS + (j + 1))
                            for k in range(QUAD):
                                wait(pe, added, g * G + (j * QUAD + k - QUAD + 1))
                                nc.tensor.matmul(window[:, k, 0:P], max_rows[j % 2][:, k, :], hot[j % 2][:, k, :], start=True, stop=True).then_inc(summed, 1)
                    steps(pe, step)

    def nodes_fifth():
        S = 5
        TURNS = turns_of(S)
        with Phase() as ctx:
            w_dst, w_self, w_agg, w_2 = (sbuf(ctx, n, [C_IN, C_IN]) for n in ("w_dst", "w_self", "w_agg", "w_2"))
            b_m, b_1 = (sbuf(ctx, n, [C_IN, 1]) for n in ("b_m", "b_1"))
            b_2 = sbuf(ctx, "b_2", [1, C_IN])
            eps = sbuf(ctx, "eps", [NT, 1])
            z_T = [sbuf(ctx, f"z_T{s}", [C_IN, NT]) for s in range(S)]
            x = [sbuf(ctx, f"x{s}", [NT, C_IN]) for s in range(S)]
            agg = [sbuf(ctx, f"agg{s}", [C_IN, NT]) for s in range(S)]
            hidden = [sbuf(ctx, f"hidden{s}", [C_IN, NT]) for s in range(S)]
            xn = [sbuf(ctx, f"xn{s}", [NT, C_IN]) for s in range(S)]
            h = [sbuf(ctx, f"h{s}", [NT, C_IN]) for s in range(S)]
            norm = [Norm(ctx, "norm", s) for s in range(S)]
            bank = [psum(ctx, f"bank{s}", [P, BANK]) for s in range(S)]
            dst_ps = [bank[s][:, 0:NT] for s in range(S)]
            hidden_ps = [bank[s][:, NT:2 * NT] for s in range(S)]
            node_ps = [bank[s][0:NT, 2 * NT:2 * NT + C_IN] for s in range(S)]
            weights_in, eps_set, steps = (sem(ctx, n) for n in ("weights_in", "eps_set", "steps"))
            z_in, x_in, stored = ([sem(ctx, f"{n}{s}") for s in range(S)] for n in ("z_in", "x_in", "stored"))
            dst_ready, agg_ready, hidden_turned, hidden_ready, updated, var_ready, std_ready, y_ready, h_ready = (
                sem(ctx, n) for n in ("dst_ready", "agg_ready", "hidden_turned", "hidden_ready", "updated",
                                      "var_ready", "std_ready", "y_ready", "h_ready"))
            LOADS, STORES = 7, 2
            with nc.Block() as block:
                @block.sync
                def _(sp):
                    load = lambda to, ap: sp.dma_start(to, ap).then_inc(weights_in, 16)
                    load(w_dst[:], t["L2_gnn_Wm"][0:C_IN, :])
                    load(w_self[:], t["L2_gnn_W1"][0:C_IN, :])
                    load(w_agg[:], t["L2_gnn_W1"][C_IN:2 * C_IN, :])
                    load(w_2[:], t["L2_gnn_W2"])
                    load(b_m[:], by_feature(t["L2_gnn_bm"]))
                    load(b_1[:], by_feature(t["L2_gnn_b1"]))
                    load(b_2[:], over_partitions(t["L2_gnn_b2"], 1))

                    def load_z(b, s):
                        sp.dma_start(z_T[s][:], h2_T[:, ds(b * NT, NT)]).then_inc(z_in[s], 16)

                    def load_x(b, s):
                        sp.dma_start(x[s][:], node_rows(x2, b)).then_inc(x_in[s], 16)
                    for s in range(S):
                        load_z(s, s)
                        load_x(s, s)

                    def turn(i):
                        more = not (isinstance(i, int) and i == TURNS - 1)

                        def after(semaphore, s):
                            wait_apart(sp, semaphore, i * S + s + 1, (weights_in, 16 * LOADS))
                        for s in range(S):
                            if more:
                                after(hidden_turned, s)
                                load_z(i * S + s + S, s)
                        for s in range(S):
                            after(var_ready, s)
                            sp.dma_start(node_rows(x3, i * S + s), xn[s][:]).then_inc(stored[s], 16)
                            if more:
                                load_x(i * S + s + S, s)
                        for s in range(S):
                            after(h_ready, s)
                            sp.dma_start(node_rows(h3_rows, i * S + s), h[s][:]).then_inc(stored[s], 16)
                    turns_loop(sp, TURNS, turn)
                    for s in range(S):
                        sp.wait_ge(stored[s], 16 * STORES * TURNS)

                @block.vector
                def _(dve):
                    chain = Chain(dve, steps, (eps_set, 1))
                    nc.vector.memset(eps[:], EPS_LN).then_inc(eps_set, 1)
                    dve.wait_ge(weights_in, 16 * LOADS)

                    def turn(i):
                        chain.turn(i)
                        for s in range(S):
                            cols = ds((i * S + s) * NT, NT)
                            dve.wait_ge(dst_ready, i * S + s + 1)
                            wait(dve, hidden_turned, i * S - S + s + 1)
                            chain.link(nc.vector.scalar_tensor_tensor(agg[s][:], dst_ps[s], b_m[:], acc[:, 0, cols], ALU.add, ALU.add))
                            nc.vector.scalar_tensor_tensor(agg[s][:], acc[:, 1, cols], 0.0, agg[s][:], ALU.is_gt, ALU.mult).then_inc(agg_ready, 1)
                        for s in range(S):
                            dve.wait_ge(updated, i * S + s + 1)
                            dve.wait_ge(x_in[s], i * 16 + 16)
                            wait(dve, stored[s], i * (16 * STORES))
                            chain.link(nc.vector.tensor_tensor(xn[s][:], node_ps[s], x[s][:], ALU.add))
                            norm[s].statistics(chain, xn[s][:]).then_inc(var_ready, 1)
                        for s in range(S):
                            dve.wait_ge(std_ready, i * S + s + 1)
                            norm[s].scale(chain, h[s][:], xn[s][:]).then_inc(y_ready, 1)
                    turns_loop(dve, TURNS, turn)

                @block.scalar
                def _(act):
                    act.wait_ge(eps_set, 1)
                    act.wait_ge(weights_in, 16 * LOADS)

                    def turn(i):
                        for s in range(S):
                            act.wait_ge(hidden_turned, i * S + s + 1)
                            wait(act, updated, i * S - S + s + 1)
                            nc.scalar.activation(hidden[s][:], hidden_ps[s], ACT.Relu, bias=b_1[:]).then_inc(hidden_ready, 1)
                        for s in range(S):
                            act.wait_ge(var_ready, i * S + s + 1)
                            norm[s].root(eps[:]).then_inc(std_ready, 1)
                        for s in range(S):
                            act.wait_ge(y_ready, i * S + s + 1)
                            nc.scalar.activation(h[s][:], h[s][:], ACT.Relu).then_inc(h_ready, 1)
                    turns_loop(act, TURNS, turn)

                @block.tensor
                def _(pe):
                    pe.wait_ge(weights_in, 16 * LOADS)

                    def turn(i):
                        for s in range(S):
                            wait(pe, var_ready, i * S - S + s + 1)
                            pe.wait_ge(z_in[s], i * 16 + 16)
                            nc.tensor.matmul(dst_ps[s], w_dst[:], z_T[s][:], start=True, stop=True).then_inc(dst_ready, 1)
                        for s in range(S):
                            pe.wait_ge(agg_ready, i * S + s + 1)
                            nc.tensor.matmul(hidden_ps[s], w_self[:], z_T[s][:], start=True, stop=False)
                            nc.tensor.matmul(hidden_ps[s], w_agg[:], agg[s][:], start=False, stop=True).then_inc(hidden_turned, 1)
                        for s in range(S):
                            pe.wait_ge(hidden_ready, i * S + s + 1)
                            nc.tensor.matmul(node_ps[s], hidden[s][:], w_2[:], start=True, stop=False)
                            nc.tensor.matmul(node_ps[s], ones[0:1, 0:NT], b_2[:], start=False, stop=True).then_inc(updated, 1)
                    turns_loop(pe, TURNS, turn)

    def edges_mean():
        with Phase() as ctx:
            passes[0] += 1
            begun = sem(ctx, "begun")
            idx = [sbuf(ctx, f"idx{n}", [P, G], i32) for n in range(SLOTS)]
            rows = [sbuf(ctx, f"rows{n}", [P, G, C_IN]) for n in range(SLOTS)]
            local = [sbuf(ctx, f"local{n}", [P, G]) for n in range(SLOTS)]
            base = sbuf(ctx, "base", [1, NCH], i32)
            hot = [sbuf(ctx, f"hot{n}", [P, QUAD, P]) for n in range(2)]
            window = psum(ctx, "window", [C_IN, QUAD, BANK])
            fixed_in = sem(ctx, "fixed_in")
            idx_in, local_in = ([sem(ctx, f"{n}{m}") for m in range(SLOTS)] for n in ("idx_in", "local_in"))
            hot_ready, summed, added = (sem(ctx, n) for n in ("hot_ready", "summed", "added"))
            with nc.Block() as block:
                @block.sync
                def _(sp):
                    sp.dma_start(base[:], win_base.rearrange("(a c) -> a c", a=1)).then_inc(fixed_in, 16)
                    groups_loop(sp, lambda g, slot: load_edges(sp, g, slot, idx, idx_in, local, dst_local, local_in, hot_ready))

                @block.gpsimd
                def _(pool):
                    pool_gathers(pool, begun, idx_in, summed, G, h3_rows, idx, rows)

                @block.vector
                def _(dve):
                    nc.vector.memset(acc[:, 0, :], 0.0).then_inc(begun, 1)
                    nc.vector.memset(acc[:, 1, :], 0.0).then_inc(begun, 1)
                    dve.wait_ge(begun, 2)
                    dve.wait_ge(fixed_in, 16)

                    def hots(g, slot, j):
                        if j == 0:
                            dve.wait_ge(local_in[slot], (uses(g, slot) + 1) * 16)
                        wait(dve, summed, (g * QUADS + (j - 1)) * QUAD)
                        one_hots(hot[j % 2][:], local[slot][:, j * QUAD:(j + 1) * QUAD]).then_inc(hot_ready, 1)

                    hots(0, 0, 0)

                    def body(g, slot):
                        for j in range(QUADS):
                            if j < QUADS - 1:
                                hots(g, slot, j + 1)
                            elif not (isinstance(g, int) and g == NG - 1):
                                hots(g + 1, (slot + 1) % SLOTS, 0)
                            at = load_bases(base, g * G + j * QUAD, QUAD, DVE_ONLY)
                            for k in range(QUAD):
                                dve.wait_ge(summed, g * G + (j * QUAD + k + 1))
                                wait(dve, added, g * G + (j * QUAD + k))
                                win = acc[:, :, ds(at[k], P)]
                                nc.vector.tensor_tensor(win, win, window[:, k, 0:2 * P].rearrange("f (a n) -> f a n", a=2),
                                                        ALU.add).then_inc(added, 1)
                    groups_loop(dve, body)

                @block.tensor
                def _(pe):
                    pe.wait_ge(begun, 1)

                    def body(g, slot):
                        for k in range(G):
                            j = k // QUAD
                            if k % QUAD == 0:
                                pe.wait_ge(rows_in[slot][j], gathered(g, slot) + 16 * QUAD)
                                pe.wait_ge(hot_ready, g * QUADS + (j + 1))
                            wait(pe, added, g * G + (k - QUAD + 1))
                            edges = hot[j % 2][:, k % QUAD, :]
                            nc.tensor.matmul(window[:, k % QUAD, 0:P], rows[slot][:, k, :], edges, start=True, stop=True)
                            nc.tensor.matmul(window[:, k % QUAD, P:2 * P], ones, edges, start=True, stop=True).then_inc(summed, 1)
                    groups_loop(pe, body)

    def nodes_last():
        S = 5
        TURNS = turns_of(S)
        with Phase() as ctx:
            x = [sbuf(ctx, f"x{s}", [NT, C_IN]) for s in range(S)]
            count = [sbuf(ctx, f"count{s}", [C_IN, NT]) for s in range(S)]
            mean = [sbuf(ctx, f"mean{s}", [C_IN, NT]) for s in range(S)]
            xn = [sbuf(ctx, f"xn{s}", [NT, C_IN]) for s in range(S)]
            mean_ps = [psum(ctx, f"mean_ps{s}", [NT, C_IN]) for s in range(S)]
            steps = sem(ctx, "steps")
            x_in, stored = ([sem(ctx, f"{n}{s}") for s in range(S)] for n in ("x_in", "stored"))
            mean_ready, turned, out_ready = (sem(ctx, n) for n in ("mean_ready", "turned", "out_ready"))
            with nc.Block() as block:
                @block.sync
                def _(sp):
                    def load_x(b, s):
                        sp.dma_start(x[s][:], node_rows(x3, b)).then_inc(x_in[s], 16)
                    for s in range(S):
                        load_x(s, s)

                    def turn(i):
                        for s in range(S):
                            sp.wait_ge(out_ready, i * S + s + 1)
                            sp.wait_ge(x_in[s], 16)
                            sp.dma_start(node_rows(out, i * S + s), xn[s][:]).then_inc(stored[s], 16)
                            if not (isinstance(i, int) and i == TURNS - 1):
                                load_x(i * S + s + S, s)
                    turns_loop(sp, TURNS, turn)
                    for s in range(S):
                        sp.wait_ge(stored[s], 16 * TURNS)

                @block.vector
                def _(dve):
                    chain = Chain(dve, steps)

                    def turn(i):
                        chain.turn(i)
                        for s in range(S):
                            cols = ds((i * S + s) * NT, NT)
                            wait(dve, turned, i * S - S + s + 1)
                            chain.link(nc.vector.tensor_scalar(count[s][:], acc[:, 1, cols], 1.0, None, ALU.max))
                            chain.link(nc.vector.reciprocal(count[s][:], count[s][:]))
                            nc.vector.tensor_tensor(mean[s][:], acc[:, 0, cols], count[s][:], ALU.mult).then_inc(mean_ready, 1)
                        for s in range(S):
                            dve.wait_ge(turned, i * S + s + 1)
                            dve.wait_ge(x_in[s], i * 16 + 16)
                            wait(dve, stored[s], i * 16)
                            nc.vector.tensor_tensor(xn[s][:], mean_ps[s][:], x[s][:], ALU.add).then_inc(out_ready, 1)
                    turns_loop(dve, TURNS, turn)

                @block.tensor
                def _(pe):
                    def turn(i):
                        for s in range(S):
                            pe.wait_ge(mean_ready, i * S + s + 1)
                            wait(pe, out_ready, i * S - S + s + 1)
                            nc.tensor.transpose(mean_ps[s][:], mean[s][:], ident).then_inc(turned, 1)
                    turns_loop(pe, TURNS, turn)

    for phase in (prepare, nodes_first, edges_gat, nodes_second, edges_gat, nodes_third, edges_transformer,
                  nodes_fourth, edges_max, nodes_fifth, edges_mean, nodes_last):
        phase()
    whole.close()




_INS = ["x", "src", "dst", "edge_weight",
        "L0_gnn_W1", "L0_gnn_a_src1", "L0_gnn_a_dst1", "L0_gnn_b1",
        "L0_gnn_W2", "L0_gnn_a_src2", "L0_gnn_a_dst2", "L0_gnn_b2",
        "L1_gnn_Wq", "L1_gnn_bq", "L1_gnn_Wk", "L1_gnn_bk", "L1_gnn_Wv", "L1_gnn_bv",
        "L1_gnn_Wskip", "L1_gnn_bskip", "L1_gnn_Wo", "L1_gnn_bo", "L1_gnn_g1", "L1_gnn_b1",
        "L1_gnn_Wf1", "L1_gnn_bf1", "L1_gnn_Wf2", "L1_gnn_bf2", "L1_gnn_g2", "L1_gnn_b2",
        "L2_gnn_Wm", "L2_gnn_bm", "L2_gnn_W1", "L2_gnn_b1", "L2_gnn_W2", "L2_gnn_b2"]


def kernel(**inputs):
    import numpy as _np
    import concourse.bacc as _bacc
    from concourse import mybir as _mybir
    from concourse.bass_utils import run_bass_kernel_spmd as _run

    nc = _bacc.Bacc("TRN2", target_bir_lowering=False, num_devices=1)
    arrays, t = {}, {}
    named = [(name, _np.ascontiguousarray(inputs[name])) for name in _INS] + [("consts", constants()[0])]
    for name, a in named:
        arrays[f"in_{name}"] = a
        t[name] = nc.dram_tensor(f"in_{name}", a.shape, _mybir.dt.from_np(a.dtype), kind="ExternalInput").ap()
    out = nc.dram_tensor("out", inputs["x"].shape, _mybir.dt.float32, kind="ExternalOutput").ap()
    build(nc, t, out)
    r = _run(nc, [arrays], core_ids=[0])
    return r.results[0]["out"]
```
